# Optimizing a Trainium2 kernel written in Bass

```python
import numpy as np
import jax
import jax.numpy as jnp

def _softmax(x, axis=-1):
    return jax.nn.softmax(x, axis=axis)

def _gelu(x):
    return jax.nn.gelu(x, approximate=True)

def _silu(x):
    return jax.nn.silu(x)

def _sigmoid(x):
    return jax.nn.sigmoid(x)

def _layernorm(x, axis=-1, eps=1e-05):
    m = jnp.mean(x, axis=axis, keepdims=True)
    v = jnp.var(x, axis=axis, keepdims=True)
    return (x - m) / jnp.sqrt(v + eps)

def _scatter_add(tgt, idx, src, axis=0):
    return tgt.at[idx].add(src)

def _segment_sum(src, seg, n):
    return jax.ops.segment_sum(src, seg, n)
kernel_name = 'mk_prb_d1_jaxref_r4_4aa810'

def setup_inputs(seed: int=0):
    np.random.seed(seed)
    _w = jnp.asarray

    def _L0_attn_setup():
        import jax, jax.numpy as jnp
        import numpy as np
        B, S, HID = (1, 1024, 512)
        NH, D = (16, 128)
        RATIO, TOPK, WIN = (4, 8, 128)
        ROPE_DIM = D // 2
        EPS = 1e-06
        NEG = -1e+30

        def rmsnorm(x, w):
            return x * jax.lax.rsqrt(jnp.mean(x * x, axis=-1, keepdims=True) + EPS) * w

        def apply_rope(x, pos):
            half = ROPE_DIM // 2
            inv = 1.0 / 10000.0 ** (jnp.arange(half, dtype=x.dtype) * (2.0 / ROPE_DIM))
            ang = pos.astype(x.dtype)[:, None] * inv[None, :]
            cos, sin = (jnp.cos(ang), jnp.sin(ang))
            x1, x2, rest = (x[..., :half], x[..., half:ROPE_DIM], x[..., ROPE_DIM:])
            return jnp.concatenate([x1 * cos - x2 * sin, x1 * sin + x2 * cos, rest], axis=-1)
        key = jax.random.key(seed)
        ks = jax.random.split(key, 16)
        n = jax.random.normal
        s = 0.02
        return {'hidden_states': n(ks[0], (B, S, HID), jnp.float32), 'Wq': n(ks[1], (HID, NH * D)) * s, 'bq': jnp.zeros((NH * D,)), 'Wcmp': n(ks[2], (HID, 1)) * s, 'bcmp': jnp.zeros((1,)), 'Wk': n(ks[3], (HID, D)) * s, 'bk': jnp.zeros((D,)), 'Wv': n(ks[4], (HID, D)) * s, 'bv': jnp.zeros((D,)), 'Wlk': n(ks[5], (HID, NH * D)) * s, 'blk': jnp.zeros((NH * D,)), 'Wlv': n(ks[6], (HID, NH * D)) * s, 'blv': jnp.zeros((NH * D,)), 'qn_w': jnp.ones((D,)), 'kn_w': jnp.ones((D,)), 'Wo': n(ks[7], (NH * D, HID)) * s, 'bo': jnp.zeros((HID,))}
    _L0_attn_in = _L0_attn_setup()

    def _L0_ffn_setup():
        import jax, jax.numpy as jnp
        import numpy as np
        FP8 = jnp.float8_e4m3fn
        key = jax.random.key(seed)
        k1, k2 = jax.random.split(key)
        input1 = jax.random.normal(k1, (2, 1024, 512), dtype=jnp.float32)
        input2 = jax.random.normal(k2, (512, 512), dtype=jnp.float32)
        scale = jnp.array(0.5, dtype=jnp.float32)
        scale1 = jnp.array(0.5, dtype=jnp.float32)
        return {'input1': input1, 'input2': input2, 'scale': scale, 'scale1': scale1}
    _L0_ffn_in = _L0_ffn_setup()
    _d = {'L0_attn_hidden_states': _L0_attn_in['hidden_states'], 'L0_attn_Wq': _L0_attn_in['Wq'], 'L0_attn_bq': _L0_attn_in['bq'], 'L0_attn_Wcmp': _L0_attn_in['Wcmp'], 'L0_attn_bcmp': _L0_attn_in['bcmp'], 'L0_attn_Wk': _L0_attn_in['Wk'], 'L0_attn_bk': _L0_attn_in['bk'], 'L0_attn_Wv': _L0_attn_in['Wv'], 'L0_attn_bv': _L0_attn_in['bv'], 'L0_attn_Wlk': _L0_attn_in['Wlk'], 'L0_attn_blk': _L0_attn_in['blk'], 'L0_attn_Wlv': _L0_attn_in['Wlv'], 'L0_attn_blv': _L0_attn_in['blv'], 'L0_attn_qn_w': _L0_attn_in['qn_w'], 'L0_attn_kn_w': _L0_attn_in['kn_w'], 'L0_attn_Wo': _L0_attn_in['Wo'], 'L0_attn_bo': _L0_attn_in['bo'], 'L0_ffn_input2': _L0_ffn_in['input2'], 'L0_ffn_scale': _L0_ffn_in['scale'], 'L0_ffn_scale1': _L0_ffn_in['scale1']}
    _x0 = _d['L0_attn_hidden_states']
    _d['L0_attn_hidden_states'] = jax.random.normal(jax.random.fold_in(jax.random.key(seed), 1), (4, 1024, 512), dtype=_x0.dtype)
    del _x0
    return _d

def reference(L0_attn_hidden_states, L0_attn_Wq, L0_attn_bq, L0_attn_Wcmp, L0_attn_bcmp, L0_attn_Wk, L0_attn_bk, L0_attn_Wv, L0_attn_bv, L0_attn_Wlk, L0_attn_blk, L0_attn_Wlv, L0_attn_blv, L0_attn_qn_w, L0_attn_kn_w, L0_attn_Wo, L0_attn_bo, L0_ffn_input2, L0_ffn_scale, L0_ffn_scale1):

    def _L0_attn_ref(hidden_states, Wq, bq, Wcmp, bcmp, Wk, bk, Wv, bv, Wlk, blk, Wlv, blv, qn_w, kn_w, Wo, bo):
        import jax, jax.numpy as jnp
        import numpy as np
        B, S, HID = (1, 1024, 512)
        NH, D = (16, 128)
        RATIO, TOPK, WIN = (4, 8, 128)
        ROPE_DIM = D // 2
        EPS = 1e-06
        NEG = -1e+30

        def rmsnorm(x, w):
            return x * jax.lax.rsqrt(jnp.mean(x * x, axis=-1, keepdims=True) + EPS) * w

        def apply_rope(x, pos):
            half = ROPE_DIM // 2
            inv = 1.0 / 10000.0 ** (jnp.arange(half, dtype=x.dtype) * (2.0 / ROPE_DIM))
            ang = pos.astype(x.dtype)[:, None] * inv[None, :]
            cos, sin = (jnp.cos(ang), jnp.sin(ang))
            x1, x2, rest = (x[..., :half], x[..., half:ROPE_DIM], x[..., ROPE_DIM:])
            return jnp.concatenate([x1 * cos - x2 * sin, x1 * sin + x2 * cos, rest], axis=-1)
        Bq, Sq, _ = hidden_states.shape
        C = Sq // RATIO
        scale = 1.0 / jnp.sqrt(jnp.float32(D))
        pos = jnp.arange(Sq)
        q = (hidden_states @ Wq + bq).reshape(Bq, Sq, NH, D).transpose(0, 2, 1, 3)
        q = apply_rope(rmsnorm(q, qn_w), pos)
        w_log = (hidden_states @ Wcmp + bcmp).reshape(Bq, C, RATIO)
        w_cmp = jax.nn.softmax(w_log, axis=-1)
        entries = jnp.einsum('bcr,bcrh->bch', w_cmp, hidden_states.reshape(Bq, C, RATIO, HID))
        block_ends = jnp.arange(1, C + 1) * RATIO - 1
        ck = apply_rope(rmsnorm(entries @ Wk + bk, kn_w), block_ends)
        cv = entries @ Wv + bv
        sc = jnp.einsum('bhsd,bcd->bhsc', q, ck) * scale
        causal = block_ends[None, None, None, :] <= pos[None, None, :, None]
        sc = jnp.where(causal, sc, NEG)
        tv, ti = jax.lax.top_k(sc, TOPK)
        sel = (tv > NEG / 2).astype(sc.dtype)
        m = jnp.max(tv, axis=-1, keepdims=True)
        e = jnp.exp(tv - m) * sel
        pw = e / jnp.maximum(e.sum(axis=-1, keepdims=True), 1e-09)
        v_g = cv[jnp.arange(Bq)[:, None, None, None], ti]
        ctx_sparse = jnp.einsum('bhsk,bhskd->bhsd', pw, v_g)
        lk = apply_rope(rmsnorm((hidden_states @ Wlk + blk).reshape(Bq, Sq, NH, D).transpose(0, 2, 1, 3), kn_w), pos)
        lv = (hidden_states @ Wlv + blv).reshape(Bq, Sq, NH, D).transpose(0, 2, 1, 3)
        nc = Sq // WIN
        qc = q.reshape(Bq, NH, nc, WIN, D)

        def windowize(x):
            prev = jnp.pad(x, ((0, 0), (0, 0), (WIN, 0), (0, 0)))[:, :, :-WIN].reshape(Bq, NH, nc, WIN, D)
            cur = x.reshape(Bq, NH, nc, WIN, D)
            return jnp.concatenate([prev, cur], axis=3)
        kw, vw = (windowize(lk), windowize(lv))
        i = jnp.arange(WIN)[:, None]
        j = jnp.arange(2 * WIN)[None, :]
        rel = i + WIN - j
        band = (rel >= 0) & (rel <= WIN)
        kpos_ok = jnp.arange(nc)[:, None, None] * WIN - WIN + j[None] >= 0
        mask = band[None] & kpos_ok
        sl = jnp.einsum('bhcqd,bhckd->bhcqk', qc, kw) * scale
        sl = jnp.where(mask[None, None], sl, NEG)
        pl = jax.nn.softmax(sl, axis=-1)
        ctx_local = jnp.einsum('bhcqk,bhckd->bhcqd', pl, vw).reshape(Bq, NH, Sq, D)
        merged = (ctx_sparse + ctx_local) * 0.5
        out = merged.transpose(0, 2, 1, 3).reshape(Bq, Sq, NH * D) @ Wo + bo
        return out

    def _L0_ffn_ref(input1, input2, scale, scale1):
        import jax, jax.numpy as jnp
        import numpy as np
        FP8 = jnp.float8_e4m3fn
        q1 = (input1 * scale).astype(FP8)
        q2 = (input2 * scale1).astype(FP8)
        d1 = q1.astype(jnp.float32) * (1.0 / scale)
        d2 = q2.astype(jnp.float32) * (1.0 / scale1)
        return jnp.einsum('bmk,kn->bmn', d1, d2)
    x = L0_attn_hidden_states
    xn = _layernorm(x, axis=-1)
    x = x + _L0_attn_ref(xn, L0_attn_Wq, L0_attn_bq, L0_attn_Wcmp, L0_attn_bcmp, L0_attn_Wk, L0_attn_bk, L0_attn_Wv, L0_attn_bv, L0_attn_Wlk, L0_attn_blk, L0_attn_Wlv, L0_attn_blv, L0_attn_qn_w, L0_attn_kn_w, L0_attn_Wo, L0_attn_bo) + _L0_ffn_ref(xn, L0_ffn_input2, L0_ffn_scale, L0_ffn_scale1)
    return x

_drawn_inputs = setup_inputs


def setup_inputs(seed=0):
    import zlib

    import numpy as np

    out = dict(_drawn_inputs(seed))
    spreads = {'L0_attn_bq': (0.0, 0.8),
     'L0_attn_bk': (0.0, 0.8),
     'L0_attn_bv': (0.0, 0.8),
     'L0_attn_blk': (0.0, 0.8),
     'L0_attn_blv': (0.0, 0.8),
     'L0_attn_qn_w': (1.0, 0.6),
     'L0_attn_kn_w': (1.0, 0.6),
     'L0_attn_bo': (0.0, 0.8)}
    factors = {'L0_attn_Wq': 8.0,
     'L0_attn_Wcmp': 8.0,
     'L0_attn_Wk': 8.0,
     'L0_attn_Wv': 8.0,
     'L0_attn_Wlk': 8.0,
     'L0_attn_Wlv': 8.0,
     'L0_attn_Wo': 8.0}
    for name, (base, spread) in spreads.items():
        noise = np.random.default_rng([zlib.crc32(name.encode()), seed]).standard_normal(out[name].shape)
        drawn = base * np.exp(spread * noise) if base else spread * noise
        out[name] = jnp.asarray(drawn.astype(out[name].dtype))
    for name, factor in factors.items():
        out[name] = (out[name] * factor).astype(out[name].dtype)
    return out
```

```python
from contextlib import ExitStack

import concourse.bass as bass
from concourse import mybir

F32 = mybir.dt.float32
F32R = mybir.dt.float32r
BF16 = mybir.dt.bfloat16
F8 = mybir.dt.float8e4
ALU = mybir.AluOpType
ACT = mybir.ActivationFunctionType
AX_X = mybir.AxisListType.X

NB, SEQ, HID, NH, D = 4, 1024, 512, 16, 128
NT = SEQ // 128
KT = HID // 128
NG = NH // 2
NU = NB * NG * NT
NTT = NB * NT
NEG = -1e30
GONE = -3e38
BIG = 3.4e38
RMS_EPS = 128 * 1e-6
SQD = float(D) ** 0.5
XR, QR = 2, 6

C_ID, C_MK, C_MG, C_SEL, C_MR, C_NR, C_M32, C_N = 0, 128, 512, 640, 672, 673, 674, 706


class Queues:

    def __init__(self, sem):
        self.sem, self.ops, self.n, self.at = sem, {}, {}, {}

    def put(self, eng, fn, *waits, name=None, quiet=False):
        self.ops.setdefault(eng, []).append((fn, waits, None if quiet else eng, 1))
        if not quiet:
            self.n[eng] = self.n.get(eng, 0) + 1
        if name is not None:
            assert not quiet and name not in self.at, name
            self.at[name] = (eng, self.n[eng])

    def dma(self, fn, stream, *waits, name=None):
        self.ops.setdefault("sync", []).append((fn, waits, stream, 16))
        self.n[stream] = self.n.get(stream, 0) + 16
        if name is not None:
            self.at[name] = (stream, self.n[stream])

    def emit(self, eng, e):
        seen = {}
        for fn, waits, on, v in self.ops.get(eng, []):
            for w in waits:
                if isinstance(w[1], int) and w[1] < 0:
                    continue
                s, c = self.at[w]
                if seen.get(s, 0) < c:
                    e.wait_ge(self.sem(s), c)
                    seen[s] = c
            i = fn(e)
            if on is not None:
                i.then_inc(self.sem(on), v)
        for s in sorted(k for k in self.n if k.startswith("d_")) if eng == "sync" else []:
            e.wait_ge(self.sem(s), self.n[s])


def build(nc, x, Wq, bq, Wcmp, bcmp, Wk, bk, Wv, bv, Wlk, blk, Wlv, blv, qnw, knw, Wo, bo,
          W2, sc0, sc1, consts, tabs, ctabs, out):
    ctx = ExitStack()
    S = {}

    def sb(name, shape, dt=F32):
        return ctx.enter_context(nc.sbuf_tensor(name, shape, dt))

    def ps(name, shape):
        return ctx.enter_context(nc.psum_tensor(name, shape, F32))

    def sem(name):
        if name not in S:
            S[name] = ctx.enter_context(nc.semaphore("s_" + name))
        return S[name]

    with ctx:
        xh = sb("xh", [128, KT, SEQ], F32R)
        xl = sb("xl", [128, KT, SEQ], F32R)
        wr = sb("wr", [128, 2, 512])
        wh = sb("wh", [128, 2, KT, 768], F32R)
        wl = sb("wl", [128, 2, KT, 768], F32R)
        woh = sb("woh", [128, 2, 512], F32R)
        wol = sb("wol", [128, 2, 512], F32R)
        acc = sb("acc", [128, NT, 512])
        qkh = sb("qkh", [128, 3, 2, 2, 128], F32R)
        qkl = sb("qkl", [128, 3, 2, 2, 128], F32R)
        vh = sb("vh", [128, 4, 2, 128], F32R)
        vl = sb("vl", [128, 4, 2, 128], F32R)
        raw = sb("raw", [128, 2, 2, 2, 128])
        t1 = sb("t1", [128, 2, 2, 64])
        t2 = sb("t2", [128, 2, 2, 64])
        tA = sb("tA", [128, NT, 2, 64])
        tB = sb("tB", [128, NT, 2, 64])
        cA = sb("cA", [128, 2, 64])
        cB = sb("cB", [128, 2, 64])
        wqk = sb("wqk", [128, 64])
        P = sb("P", [128, 2, 2, 512])
        es = sb("es", [128, 2, 256])
        rp = sb("rp", [128, 2, 256])
        pth = sb("pth", [128, 2, 512], F32R)
        ptl = sb("ptl", [128, 2, 512], F32R)
        ch = sb("ch", [128, 2, 2, 128], F32R)
        cl = sb("cl", [128, 2, 2, 128], F32R)
        ckh = sb("ckh", [128, 2, 256], F32R)
        ckl = sb("ckl", [128, 2, 256], F32R)
        cvh = sb("cvh", [128, 2, 2, 128], F32R)
        cvl = sb("cvl", [128, 2, 2, 128], F32R)
        xt = sb("xt", [128, XR, 512])
        q8 = sb("q8", [128, QR, 512], BF16)
        a8 = sb("a8", [128, 512], F8)
        b8 = sb("b8", [128, 512], F8)
        qa = sb("qa", [128, 512], BF16)
        qb = sb("qb", [128, 512], BF16)
        w2q = sb("w2q", [128, KT, 512], BF16)
        et = sb("et", [128, KT, 128])
        wkv = sb("wkv", [128, KT, 256])
        bkv = sb("bkv", [1, 256])
        ckr = sb("ckr", [128, 256])
        ct = sb("ct", [128, 2, 64])
        wcb = sb("wcb", [128, 512])
        bob = sb("bob", [128, 512])
        br = sb("br", [128, 2, 2, 128])
        bh = sb("bh", [128, 2, 512], F32R)
        cst = sb("cst", [128, C_N])
        idb = sb("idb", [128, 128], BF16)
        m32 = sb("m32", [128, 32], BF16)
        onef = sb("onef", [128, 128])
        oner = sb("oner", [128, 128], F32R)
        junk = sb("junk", [128, 5, 128], BF16)
        junkd = sb("junkd", [128, 512], BF16)
        dg = sb("dg", [128, 128])
        eg = sb("eg", [128, 128])
        wm = sb("wm", [128, 32])
        sm = sb("sm", [128, 16])
        st = sb("st", [128, 12])
        mh = sb("mh", [128, 4])
        ss = sb("ss", [128, 4, 4])
        r4 = sb("r4", [128, 4, 4])
        ngr = sb("ngr", [128, 4, 2])
        mm = sb("mm", [128, 4, 2, 9])
        nm = sb("nm", [128, 4, 2, 2])
        su = sb("su", [128, 4, 2, 2])
        rs = sb("rs", [128, 4, 2, 2])
        blT = sb("blT", [128, NH])
        isc = sb("isc", [128, 5])
        bcm = sb("bcm", [128, 1])
        wrow = P[:, 1, 0, 0:256]

        bQK = ps("bQK", [128, 512])
        bVC = ps("bVC", [128, 512])
        bT = ps("bT", [128, 512])
        bS = [ps("bS0", [128, 512]), ps("bS1", [128, 512])]
        bP = [ps("bP0", [128, 512]), ps("bP1", [128, 512])]
        bY = ps("bY", [128, 512])

        ident = cst[:, C_ID:C_ID + 128]

        def flat(ap):
            return ap.rearrange("p a b c -> p (a b c)")

        def f32(ap):
            return ap.bitcast(F32)

        qu = Queues(sem)
        put, dma = qu.put, qu.dma
        PE, AC, DV, PO = "tensor", "scalar", "vector", "gpsimd"

        def slots_of(u):
            s = u % 3
            return [s] if u % 8 == 0 else [0, 2] if s == 0 else [s - 1, s]

        def units_of(u):
            return [u] if u % 8 == 0 else [u, u - 1] if u % 3 == 0 else [u - 1, u]

        def mask_of(u):
            a = C_MK + (0 if u % 3 == 0 or u % 8 == 0 else 128)
            return cst[:, a:a + nloc(u)]

        def width(u):
            return 32 * (u % 8 + 1)

        def nloc(u):
            return 128 if u % 8 == 0 else 256

        def pblocks(u):
            return ([0] if u % 8 == 0 else [0, 1]) + ([2] if u % 8 < 4 else [2, 3])

        chunks = []
        for s in range(-8, NU):
            gi, i = s // 8, s % 8
            if i == 3 and gi >= 0:
                chunks += [("o", gi, 0, s), ("o", gi, 1, s)]
            if i != 3 and i != 7 and gi + 1 < NU // 8:
                chunks.append(("w", gi + 1, i if i < 3 else i - 1, s))
        where = {(k, gi, c): q for q, (k, gi, c, _) in enumerate(chunks)}

        def load_x(t):
            dma(lambda e: e.dma_start(xt[:, t % XR, :], x[t // 8, (t % 8) * 128:(t % 8 + 1) * 128, :]),
                f"d_x{t % XR}", ("et", t - XR), name=("x", t))

        def load_chunk(q):
            k, gi, c, _ = chunks[q]
            g = gi % NG
            free = [("wohi", q - 2), ("wolo", q - 2)] if q >= 2 and chunks[q - 2][0] == "o" else [("split", q - 2)]
            dst, stream = wr[:, q % 2, :], f"d_w{q % 2}"
            if k == "o":
                h = 2 * g + c
                dma(lambda e: e.dma_start(dst, Wo[h * 128:(h + 1) * 128, :]), stream, *free, name=("w", q))
            elif c < 4:
                d4 = dst.rearrange("p (h k d) -> p h k d", h=2, k=2)
                for j, w in enumerate((Wq, Wlk)):
                    src = w[c * 128:(c + 1) * 128, g * 256:(g + 1) * 256].rearrange("p (h d) -> p h d", h=2)
                    dma(lambda e, j=j, src=src: e.dma_start(d4[:, :, j, :], src), stream, *free,
                        name=("w", q) if j else None)
            else:
                k0 = 2 * (c - 4)
                src = Wlv[k0 * 128:(k0 + 2) * 128, g * 256:(g + 1) * 256].rearrange("(k p) n -> p k n", p=128)
                dma(lambda e: e.dma_start(dst.rearrange("p (k n) -> p k n", k=2), src), stream, *free,
                    name=("w", q))

        def load_bias(gi):
            g = gi % NG
            for j, w in enumerate((bq, blk)):
                for h in range(2):
                    o = g * 256 + h * 128
                    src = w[o:o + 128].rearrange("(a d) -> a d", a=1).broadcast_to([128, 128])
                    dma(lambda e, h=h, j=j, src=src: e.dma_start(br[:, h, j, :], src), "d_b", ("bias", gi - 1),
                        name=("br", gi) if h + j == 2 else None)

        def bc(ap, n):
            return ap.rearrange("(a n) -> a n", a=1).broadcast_to([128, n])

        def first_loads():
            def load(stream, dst, src, name=None, **kw):
                dma(lambda e: e.dma_start(dst, src, **kw), stream, name=name)

            load("d_c", cst[:, :], consts)
            load("d_c", wcb[:, :], Wcmp.rearrange("n a -> a n").broadcast_to([128, 512]))
            load("d_c", bcm[:, :], bc(bcmp, 1))
            load("d_c", isc[:, 0:1], bc(sc0, 1))
            load("d_c", isc[:, 1:2], bc(sc1, 1), name=("const", 0))
            load_x(0)
            load("d_2", acc[:, 0:KT, :], W2.rearrange("(k p) n -> p k n", p=128), name=("w2raw", 0))
            load_chunk(0)
            load_x(1)
            load("d_t", wrow[:, 0:128], bc(qnw, 128))
            load("d_t", wrow[:, 128:256], bc(knw, 128))
            for j in range(2):
                load("d_t", tA[:, :, j, :], tabs[0])
                load("d_t", tB[:, :, j, :], tabs[1])
            load("d_t", cA[:, :, :], ctabs[0])
            load("d_t", cB[:, :, :], ctabs[1])
            load("d_t", wkv[:, :, 0:128], Wk.rearrange("(k p) n -> p k n", p=128))
            load("d_t", wkv[:, :, 128:256], Wv.rearrange("(k p) n -> p k n", p=128))
            load("d_t", bkv[:, 0:128], bk.rearrange("(a n) -> a n", a=1))
            load("d_t", bkv[:, 128:256], bv.rearrange("(a n) -> a n", a=1))
            load("d_t", bob[:, :], bc(bo, 512))
            load("d_t", blT[:, :], blv.rearrange("(h d) -> d h", d=128), name=("table", 0),
                 allow_slow_non_contiguous=True)
            load_bias(0)

        def load_acc(t):
            wait = ("store", t - 8) if t >= 8 else ("w2", KT - 1)
            dma(lambda e: e.dma_start(acc[:, t % 8, :], x[t // 8, (t % 8) * 128:(t % 8 + 1) * 128, :]),
                f"d_a{t % 8}", wait, name=("xacc", t))

        def store(u):
            b, i = u // 64, u % 8
            dma(lambda e: e.dma_start(out[b, i * 128:(i + 1) * 128, :], acc[:, i, :]), f"d_o{i}", ("acc", u),
                name=("store", b * 8 + i))

        free = {"T": [], "Y": []}

        def mm_(dst, a, b, start, stop, *waits, name=None):
            put(PE, lambda e: e.matmul(dst, a, b, start=start, stop=stop), *waits, name=name, quiet=name is None)

        def turn_(dst, src, *waits, name=None):
            put(PE, lambda e: e.transpose(dst, src, ident), *waits, name=name, quiet=name is None)

        def three(dst, ah, al, bh_, bl_, first, last, *waits, name=None):
            mm_(dst, ah, bh_, first, False, *waits)
            mm_(dst, ah, bl_, False, False)
            mm_(dst, al, bh_, False, last, name=name)

        def tr(u):
            for k in range(4):
                turn_(bT[:, k * 128:(k + 1) * 128], raw[:, u % 2, k // 2, k % 2, :], ("kscale", u), ("const", 0),
                      *free["T"], name=("tr", u) if k == 3 else None)
            free["T"] = [("hi_qk", u), ("lo_qk", u)]

        def proj_qk(u):
            gi, i, w = u // 8, u % 8, u // 8 % 2
            waits = [("sq", u - 1), ("split", where["w", gi, 3]), ("bias", gi)]
            if gi % NG == 0:
                waits += [("hi_x", u // 64 * 8 + i), ("lo_x", u // 64 * 8 + i)]
            c = slice(i * 128, (i + 1) * 128)
            for kt in range(KT):
                three(bQK[:, :], xh[:, kt, c], xl[:, kt, c], wh[:, w, kt, 0:512], wl[:, w, kt, 0:512],
                      kt == 0, False, *waits)
            mm_(bQK[:, :], oner[:, :], bh[:, w, :], False, True, name=("qk", u))

        def proj_v(u):
            gi, i, w = u // 8, u % 8, u // 8 % 2
            waits = [("hi_c", u - 3), ("lo_c", u - 3), ("hi_v", u - 1), ("lo_v", u - 1),
                     ("split", where["w", gi, 5])]
            c = slice(i * 128, (i + 1) * 128)
            for kt in range(KT):
                three(bVC[:, 0:256], xh[:, kt, c], xl[:, kt, c], wh[:, w, kt, 512:768], wl[:, w, kt, 512:768],
                      kt == 0, kt == KT - 1, *waits, name=("v", u) if kt == KT - 1 else None)

        def scores(u, h):
            b, i, C = u // 64, u % 8, width(u)
            k = 2 * b + i // 4
            waits = [("hi_qk", u), ("lo_qk", u), ("hi_ck", k), ("lo_ck", k), ("mr", 2 * (u - 1) + h),
                     ("es", 2 * (u - 1) + h)]
            sl = slots_of(u)
            keys = slice(sl[0], sl[-1] + 1, max(sl[-1] - sl[0], 1))
            q_, ql_ = qkh[:, u % 3, h, 0, :], qkl[:, u % 3, h, 0, :]
            three(bS[h][:, 0:nloc(u)], q_, ql_, qkh[:, keys, h, 1, :], qkl[:, keys, h, 1, :], True, True, *waits)
            cmp = bS[h][:, 256:256 + C]
            mm_(cmp, q_, ckh[:, b % 2, 0:C], True, False)
            mm_(cmp, q_, ckl[:, b % 2, 0:C], False, False)
            mm_(bS[h][:, 256 + C - 32:256 + C], idb[:, :], m32[:, :], False, False)
            mm_(cmp, ql_, ckh[:, b % 2, 0:C], False, True, name=("s", 2 * u + h))

        def turn_p(u, h):
            a = 2 * u + h
            bl = pblocks(u)
            for n, k in enumerate(bl):
                turn_(bP[h][:, n * 128:(n + 1) * 128], P[:, u % 2, h, k * 128:(k + 1) * 128], ("norm", a),
                      ("hi_p", a - 2), ("lo_p", a - 2), name=("pt", a) if n == len(bl) - 1 else None)

        def values(u, h):
            a, b, i = 2 * u + h, u // 64, u % 8
            k = 2 * b + i // 4
            waits = [("hi_p", a), ("lo_p", a), ("hi_v", u), ("lo_v", u), ("hi_cv", k), ("lo_cv", k),
                     ("hi_c", u - 1), ("lo_c", u - 1)]
            vals = [(vh[:, t % 4, h, :], vl[:, t % 4, h, :]) for t in units_of(u)]
            vals += [(cvh[:, b % 2, n, :], cvl[:, b % 2, n, :]) for n in range(i // 4 + 1)]
            for n, (v_, vl_) in enumerate(vals):
                c = slice(n * 128, (n + 1) * 128)
                last = n == len(vals) - 1
                three(bVC[:, 256 + h * 128:384 + h * 128], v_, vl_, pth[:, h, c], ptl[:, h, c], n == 0, last,
                      *waits, name=("c", a) if last else None)

        def out_proj(u):
            gi = u // 8
            waits = [("hi_c", u), ("lo_c", u), ("wolo", where["o", gi, 1]), ("wohi", where["o", gi, 1])]
            for h in range(2):
                three(bY[:, :], ch[:, u % 2, h, :], cl[:, u % 2, h, :], woh[:, h, :], wol[:, h, :], h == 0, h == 1,
                      *waits, *free["Y"], name=("wo", u) if h else None)
            free["Y"] = [("acc", u)]

        def turn_x(t):
            for kt in range(KT):
                turn_(bT[:, kt * 128:(kt + 1) * 128], xt[:, t % XR, kt * 128:(kt + 1) * 128], ("xn", t),
                      *free["T"], name=("xt", t) if kt == KT - 1 else None)
            free["T"] = [("b8", t), ("lo_x", t)]
            mm_(bY[:, 0:128], onef[:, :], dg[:, :], True, True, ("dg", t), *free["Y"], name=("bc", t))
            free["Y"] = [("eg", t)]

        def entries(t):
            for kt in range(KT):
                mm_(bY[:, kt * 32:(kt + 1) * 32], xt[:, t % XR, kt * 128:(kt + 1) * 128], wm[:, :], True, True,
                    ("wm", t), *free["Y"], name=("et", t) if kt == KT - 1 else None)
            free["Y"] = [("put_et", t)]

        def ckv(k):
            for kt in range(KT):
                mm_(bY[:, 0:256], et[:, kt, :], wkv[:, kt, :], kt == 0, False, ("put_et", 4 * k + 3), *free["Y"])
            mm_(bY[:, 0:256], onef[0:1, :], bkv[:, :], False, True, name=("kv", k))
            free["Y"] = [("css", k)]

        def turn_ck(k):
            turn_(bT[:, 0:128], ckr[:, 0:128], ("cks", k), *free["T"], name=("ct", k))
            free["T"] = [("hi_ck", k), ("lo_ck", k)]

        def ffn(t):
            for kt in range(KT):
                mm_(bY[:, :], q8[:, t % QR, kt * 128:(kt + 1) * 128], w2q[:, kt, :], kt == 0, kt == KT - 1,
                    ("q8", t), *free["Y"], name=("ff", t) if kt == KT - 1 else None)
            free["Y"] = [("init", t)]

        def act(dst, src, func, *waits, name=None, **kw):
            put(AC, lambda e: e.activation(dst, src, func, **kw), *waits, name=name)

        def hi_qk(u):
            act(flat(qkh[:, u % 3]), bT[:, :], ACT.Copy, ("tr", u), ("s", 2 * (u - 2) + 1), ("lo_qk", u - 3),
                name=("hi_qk", u))

        def hi_p(u, h):
            n = len(pblocks(u)) * 128
            act(pth[:, h, 0:n], bP[h][:, 0:n], ACT.Copy, ("pt", 2 * u + h), ("c", 2 * (u - 1) + h),
                name=("hi_p", 2 * u + h))

        def evac_qk(u):
            act(flat(raw[:, u % 2]), bQK[:, :], ACT.Copy, ("qk", u), ("tr", u - 2), name=("raw", u))

        def squares(u):
            for k in range(4):
                act(junk[:, k, :], bQK[:, k * 128:(k + 1) * 128], ACT.Square, ("sq", u - 1),
                    accum_out=ss[:, u % 4, k:k + 1], name=("sq", u) if k == 3 else None)

        def exps(u):
            for h in range(2):
                pl = P[:, u % 2, h, 0:nloc(u)]
                act(pl, pl, ACT.Exp, ("nm", u), scale=r4[:, u % 4, 2 * h:2 * h + 1], bias=nm[:, u % 4, h, 1:2],
                    accum_out=su[:, u % 4, h, 1:2], name=("el", 2 * u + h))
            for h in range(2):
                C = width(u)
                act(es[:, h, 0:C], bS[h][:, 256:256 + C], ACT.Exp, ("stt", 2 * (u - 1) + h),
                    scale=r4[:, u % 4, 2 * h:2 * h + 1], bias=nm[:, u % 4, h, 0:1], name=("es", 2 * u + h))

        def hi_v(u):
            act(vh[:, u % 4].rearrange("p a b -> p (a b)"), bVC[:, 0:256], ACT.Copy, ("v", u),
                ("c", 2 * (u - 2) + 1), name=("hi_v", u))

        def hi_c(u):
            g = (u // 8) % 8
            for h in range(2):
                act(ch[:, u % 2, h, :], bVC[:, 256 + h * 128:384 + h * 128], ACT.Identity, ("c", 2 * u + 1),
                    ("wo", u - 2), ("bl", 0), bias=blT[:, 2 * g + h:2 * g + h + 1], name=("hi_c", u) if h else None)

        def hi_wo(q):
            gi, c = chunks[q][1:3]
            act(woh[:, c, :], wr[:, q % 2, :], ACT.Copy, ("w", q), ("wo", 8 * gi - 1), name=("wohi", q))

        def hi_x(t):
            b, j = t // 8, t % 8
            src = bT[:, :].rearrange("p (k c) -> p k c", k=KT)
            act(xh[:, :, j * 128:(j + 1) * 128], src, ACT.Copy, ("xt", t), ("v", (b - 1) * 64 + 56 + j),
                name=("hi_x", t))

        def cast8(src, i, *waits, name):
            act(a8[:, :], src, ACT.Copy, *waits, scale=isc[:, i:i + 1], saturate=False)
            act(b8[:, :], src, ACT.Copy, scale=isc[:, i + 2:i + 3], saturate=False, name=name)

        def exp_w(t):
            act(eg[:, :], eg[:, :], ACT.Exp, ("neg", t), bias=sm[:, 3:4], accum_out=sm[:, 4:5])
            act(sm[:, 5:6], sm[:, 2:3], ACT.Exp, bias=sm[:, 3:4], name=("ew", t))

        def put_et(t):
            act(et[:, :, (t % 4) * 32:(t % 4 + 1) * 32], bY[:, 0:128].rearrange("p (k c) -> p k c", k=KT),
                ACT.Copy, ("et", t), ("kv", t // 4 - 1), name=("put_et", t))

        def put_kv(k):
            b = k // 2
            act(ckr[:, :], bY[:, 0:256], ACT.Copy, ("kv", k), ("ct", k - 1), ("lo_cv", k - 1), name=("kvr", k))
            act(cvh[:, b % 2, k % 2, :], bY[:, 128:256], ACT.Copy, ("c", 2 * (64 * (b - 1) - 1) + 1),
                name=("hi_cv", k))
            act(junk[:, 4, :], bY[:, 0:128], ACT.Square, ("css", k - 1), accum_out=sm[:, 12:13], name=("css", k))

        def hi_ck(k):
            b = k // 2
            act(ckh[:, b % 2, (k % 2) * 128:(k % 2 + 1) * 128], bT[:, 0:128], ACT.Copy, ("ct", k),
                ("s", 2 * (64 * (b - 1) - 1) + 1), name=("hi_ck", k))

        def tt(eng, dst, a, b, op, *waits, name=None):
            put(eng, lambda e: e.tensor_tensor(dst, a, b, op), *waits, name=name)

        def ts(eng, dst, a, s1, s2, op0, op1, *waits, name=None, **kw):
            put(eng, lambda e: e.tensor_scalar(dst, a, s1, s2, op0, op1, **kw), *waits, name=name)

        def stt(dst, a, s, b, op0, op1, *waits, name=None, **kw):
            put(DV, lambda e: e.scalar_tensor_tensor(out=dst, in0=a, scalar=s, in1=b, op0=op0, op1=op1, **kw),
                *waits, name=name)

        def lo(dst, src, hi, *waits, name):
            tt(DV, dst, src, f32(hi), ALU.subtract, *waits, name=name)

        def lo_qk(u):
            lo(flat(qkl[:, u % 3]), bT[:, :], flat(qkh[:, u % 3]), ("hi_qk", u), ("lo_qk", u - 1), name=("lo_qk", u))

        def pick(u, h):
            C = width(u)
            stt(P[:, u % 2, h, 256:256 + C], rp[:, h, 0:C], GONE, es[:, h, 0:C], ALU.is_equal, ALU.mult,
                ("es", 2 * u + h), ("mr", 2 * u + h), ("pt", 2 * (u - 2) + h), accum_out=su[:, u % 4, h, 0:1],
                name=("stt", 2 * u + h))

        def sums(u):
            ts(DV, rs[:, u % 4], su[:, u % 4], 1e-9, None, ALU.max, ALU.bypass, ("stt", 2 * u + 1),
               ("el", 2 * u + 1), name=("rs0", u))
            put(DV, lambda e: e.reciprocal(rs[:, u % 4], rs[:, u % 4]), ("rs0", u), name=("rs", u))

        def lo_p(u, h):
            n = len(pblocks(u)) * 128
            a = 2 * u + h
            lo(ptl[:, h, 0:n], bP[h][:, 0:n], pth[:, h, 0:n], ("hi_p", a), ("lo_p", a - 2), name=("lo_p", a))

        def rope_a(u):
            b_ = [128, 2, 2, 64]
            tt(DV, t1[:, :, :, :], raw[:, u % 2, :, :, 0:64], tA[:, u % 8].unsqueeze(1).broadcast_to(b_), ALU.mult,
               ("raw", u), ("tab", 0), ("add", u - 1), name=("t1", u))
            kr = raw[:, u % 2, :, 1, 64:128]
            tt(DV, kr, kr, wqk[:, :].unsqueeze(1).broadcast_to([128, 2, 64]), ALU.mult, name=("krest", u))

        def eps_qk(u):
            ts(DV, ss[:, u % 4], ss[:, u % 4], RMS_EPS, None, ALU.add, ALU.bypass, ("sq", u), name=("veps", u))

        def rope_add(u):
            tt(DV, raw[:, u % 2, :, :, 0:64], t1[:, :, :, :], t2[:, :, :, :], ALU.add, ("t1", u), ("t2", u),
               name=("add", u))

        def kscale(u):
            for h in range(2):
                k_ = raw[:, u % 2, h, 1, :]
                ts(DV, k_, k_, r4[:, u % 4, 2 * h + 1:2 * h + 2], SQD, ALU.mult, ALU.mult, ("r4", u), ("add", u),
                   ("krest", u), name=("kscale", u) if h else None)
            ts(DV, ngr[:, u % 4], r4[:, u % 4, 0:4:2], -1.0, None, ALU.mult, ALU.bypass, name=("ngr", u))

        def top(u, h):
            C, a = width(u), 2 * u + h
            sp, sl_ = bS[h][:, 256:256 + C], bS[h][:, 0:nloc(u)]
            m = mm[:, u % 4, h, :]
            put(DV, lambda e: e.max(m[:, 0:8], sp), ("s", a), name=("m8", a))
            pd = P[:, u % 2, h, 0:nloc(u)]
            put(DV, lambda e: e.tensor_tensor_reduce(pd, sl_, mask_of(u), 1.0, GONE, ALU.add, ALU.max, m[:, 8:9]),
                ("pt", 2 * (u - 2) + h), name=("ttr", a))
            put(DV, lambda e: e.match_replace(rp[:, h, 0:C], m[:, 0:8], sp, GONE), ("m8", a), ("stt", a - 2),
                name=("mr", a))

        def neg_max(u):
            stt(nm[:, u % 4], mm[:, u % 4, :, 0:9:8], NEG / 10, ngr[:, u % 4].unsqueeze(2).broadcast_to([128, 2, 2]),
                ALU.max, ALU.mult, ("mr", 2 * u + 1), ("ngr", u), name=("nm", u))

        def lo_v(u):
            fl_ = lambda a: a[:, u % 4].rearrange("p a b -> p (a b)")
            lo(fl_(vl), bVC[:, 0:256], fl_(vh), ("hi_v", u), ("hi_c", u - 2), ("lo_v", u - 1), name=("lo_v", u))

        def lo_c(u):
            g = (u // 8) % 8
            for h in range(2):
                stt(cl[:, u % 2, h, :], bVC[:, 256 + h * 128:384 + h * 128], blT[:, 2 * g + h:2 * g + h + 1],
                    f32(ch[:, u % 2, h, :]), ALU.add, ALU.subtract, ("hi_c", u), ("lo_c", u - 1),
                    name=("lo_c", u) if h else None)

        def add_out(u):
            a = acc[:, u % 8, :]
            first = [("init", u // 64 * 8 + u % 8)] if (u // 8) % 8 == 0 else [("acc", u - 8)]
            tt(DV, a, bY[:, :], a, ALU.add, ("wo", u), *first, name=("acc", u))

        def lo_wo(q):
            c = chunks[q][2]
            lo(wol[:, c, :], wr[:, q % 2, :], woh[:, c, :], ("wohi", q), name=("wolo", q))

        def norm_stats(t):
            xs = xt[:, t % XR, :]
            put(DV, lambda e: e.bn_stats(st[:, 0:6], xs), ("x", t), ("xn", t - 1), name=("bs", t))
            put(DV, lambda e: e.bn_aggr(st[:, 6:8], st[:, 0:6]), ("bs", t), name=("ba", t))
            ts(DV, st[:, 8:9], st[:, 7:8], 1e-5, None, ALU.add, ALU.bypass, ("ba", t), ("rstd", t - 1), name=("xv", t))

        def normalise(t):
            xs = xt[:, t % XR, :]
            ts(DV, xs, xs, st[:, 6:7], st[:, 9:10], ALU.subtract, ALU.mult, ("rstd", t), ("ba", t), name=("xn", t))
            put(DV, lambda e: e.tensor_tensor_reduce(junkd[:, :], xs, wcb[:, :], 1.0, 0.0, ALU.mult, ALU.add,
                                                     sm[:, 0:1]), ("xn", t), ("wl", t - 1), name=("wl", t))
            ts(DV, sm[:, 2:3], sm[:, 0:1], bcm[:, 0:1], None, ALU.add, ALU.bypass, ("wl", t), ("ew", t - 1),
               name=("wlb", t))
            ts(DV, dg[:, :], ident, sm[:, 2:3], None, ALU.mult, ALU.bypass, ("wlb", t), ("bc", t - 1),
               name=("dg", t))

        def lo_x(t):
            j = t % 8
            c = slice(j * 128, (j + 1) * 128)
            lo(xl[:, :, c], bT[:, :].rearrange("p (k c) -> p k c", k=KT), xh[:, :, c], ("b8", t), name=("lo_x", t))

        def group_max(t):
            put(DV, lambda e: e.tensor_tensor_reduce(eg[:, :], bY[:, 0:128], cst[:, C_MG:C_MG + 128], 1.0, GONE,
                                                     ALU.add, ALU.max, sm[:, 9:10]),
                ("bc", t), ("ew", t - 1), name=("eg", t))
            ts(DV, sm[:, 3:4], sm[:, 9:10], -1.0, None, ALU.mult, ALU.bypass, ("eg", t), name=("neg", t))

        def quant(dst, i, *waits, name):
            ts(DV, qa[:, :], a8[:, :], 240.0, -240.0, ALU.min, ALU.max, *waits)
            ts(DV, qb[:, :], b8[:, :], 120.0, -120.0, ALU.min, ALU.max, name=("qb", name))
            tt(DV, qb[:, :], b8[:, :], qb[:, :], ALU.subtract, ("qb", name), name=("qd", name))
            stt(dst, qb[:, :], 2.0, qa[:, :], ALU.mult, ALU.add, ("qd", name), name=("qs", name))
            ts(DV, qb[:, :], dst, BIG / 450.0, 0.0, ALU.mult, ALU.mult, ("qs", name), name=("qn", name))
            tt(DV, dst, dst, qb[:, :], ALU.add, ("qn", name), name=name)

        def weights4(t):
            put(DV, lambda e: e.reciprocal(sm[:, 10:11], sm[:, 4:5]), ("ew", t), name=("re", t))
            tt(DV, sm[:, 11:12], sm[:, 10:11], sm[:, 5:6], ALU.mult, ("re", t), name=("w", "tok", t))
            ts(DV, wm[:, :], cst[:, C_SEL:C_SEL + 32], sm[:, 11:12], None, ALU.mult, ALU.bypass, ("w", "tok", t),
               ("et", t - 1), name=("wm", t))

        def init(t):
            a = acc[:, t % 8, :]
            stt(a, bY[:, :], isc[:, 4:5], a, ALU.mult, ALU.add, ("ff", t), ("bo", t), ("isc", 0), name=("init", t))

        def rope_ck(k):
            ts(DV, sm[:, 13:14], sm[:, 12:13], RMS_EPS, None, ALU.add, ALU.bypass, ("css", k), name=("cke", k))
            tt(DV, ct[:, 0, :], ckr[:, 0:64], cA[:, k % 2, :], ALU.mult, ("kvr", k), ("tab", 0), ("cadd", k - 1))
            tt(DV, ct[:, 1, 0:32], ckr[:, 32:64], cB[:, k % 2, 0:32], ALU.mult)
            tt(DV, ct[:, 1, 32:64], ckr[:, 0:32], cB[:, k % 2, 32:64], ALU.mult, name=("cm", k))
            tt(DV, ckr[:, 64:128], ckr[:, 64:128], wqk[:, :], ALU.mult, name=("crest", k))
            tt(DV, ckr[:, 0:64], ct[:, 0, :], ct[:, 1, :], ALU.add, ("cm", k), name=("cadd", k))
            ts(DV, ckr[:, 0:128], ckr[:, 0:128], sm[:, 14:15], SQD, ALU.mult, ALU.mult, ("ckp", k), ("cadd", k),
               ("crest", k), name=("cks", k))
            lo(cvl[:, (k // 2) % 2, k % 2, :], ckr[:, 128:256], cvh[:, (k // 2) % 2, k % 2, :], ("hi_cv", k),
               name=("lo_cv", k))

        def lo_ck(k):
            b, c = k // 2, slice((k % 2) * 128, (k % 2 + 1) * 128)
            lo(ckl[:, b % 2, c], bT[:, 0:128], ckh[:, b % 2, c], ("hi_ck", k), name=("lo_ck", k))

        def power(dst, src, *waits, name):
            tt(PO, dst, src, mh[:, 0:src.shape[1]], ALU.pow, *waits, name=name)

        def normalise_p(u, h):
            C, top_ = width(u), 128 * (u % 8 // 4 + 1)
            if h == 0 and C < top_:
                put(PO, lambda e: e.memset(P[:, u % 2, :, 256 + C:256 + top_], 0.0), ("pt", 2 * (u - 2) + 1))
            pl, pc = P[:, u % 2, h, 0:nloc(u)], P[:, u % 2, h, 256:256 + C]
            ts(PO, pl, pl, rs[:, u % 4, h, 1:2], 0.5, ALU.mult, ALU.mult, ("rs", u))
            ts(PO, pc, pc, rs[:, u % 4, h, 0:1], 0.5, ALU.mult, ALU.mult, name=("norm", 2 * u + h))

        def rope_b(u):
            for k in range(2):
                d_, s_ = slice(32 * k, 32 * k + 32), slice(32 - 32 * k, 64 - 32 * k)
                tt(PO, t2[:, :, :, d_], raw[:, u % 2, :, :, s_],
                   tB[:, u % 8, :, d_].unsqueeze(1).broadcast_to([128, 2, 2, 32]), ALU.mult, ("raw", u), ("tab", 0),
                   ("add", u - 1), name=("t2", u) if k else None)

        def split(q):
            _, gi, c, _ = chunks[q]
            w = gi % 2
            if c < 4:
                h_, l_, src = wh[:, w, c, 0:512], wl[:, w, c, 0:512], wr[:, q % 2, :]
            else:
                k0 = 2 * (c - 4)
                h_, l_ = wh[:, w, k0:k0 + 2, 512:768], wl[:, w, k0:k0 + 2, 512:768]
                src = wr[:, q % 2, :].rearrange("p (k n) -> p k n", k=2)
            ts(PO, h_, src, 1.0, 1.0, ALU.mult, ALU.mult, ("w", q), ("v", 8 * (gi - 1) - 1), name=("sh", q))
            tt(PO, l_, src, f32(h_), ALU.subtract, ("sh", q), name=("split", q))

        def bias_rows(gi):
            b_, r_ = bh[:, gi % 2, :], flat(br)
            ts(PO, b_, r_, 1.0, 1.0, ALU.mult, ALU.mult, ("br", gi), ("qk", 8 * (gi - 1) - 1), ("const", 0),
               name=("bhi", gi))
            ts(PO, r_, r_, cst[:, C_NR:C_NR + 1], 1.0, ALU.mult, ALU.mult, ("bhi", gi), name=("bn", gi))

        def bias_done(gi):
            b_ = bh[:, gi % 2, :]
            stt(b_, f32(b_), cst[:, C_MR:C_MR + 1], flat(br), ALU.mult, ALU.add, ("bn", gi), name=("bias", gi))

        def add_bo(t):
            a = acc[:, t % 8, :]
            tt(PO, a, a, bob[:, :], ALU.add, ("xacc", t), ("table", 0), name=("bo", t))

        first_loads()
        put(PO, lambda e: e.memset(onef[:, :], 1.0))
        put(PO, lambda e: e.memset(mh[:, :], -0.5), name=("ones", 0))
        put(DV, lambda e: e.tensor_copy(oner[:, :], onef[:, :]), ("ones", 0), ("const", 0))
        put(DV, lambda e: e.tensor_copy(idb[:, :], ident))
        put(DV, lambda e: e.tensor_copy(m32[:, :], cst[:, C_M32:C_M32 + 32]))
        ts(DV, isc[:, 2:4], isc[:, 0:2], 0.5, None, ALU.mult, ALU.bypass, name=("half", 0))
        put(DV, lambda e: e.reciprocal(sm[:, 14:16], isc[:, 0:2]), name=("rsc", 0))
        tt(DV, isc[:, 4:5], sm[:, 14:15], sm[:, 15:16], ALU.mult, ("rsc", 0), name=("isc", 0))

        def quant_w2():
            for kt in range(KT):
                cast8(acc[:, kt, :], 1, ("w2raw", 0), ("half", 0), *([("w2", kt - 1)] if kt else []),
                      name=("c8", kt))
                quant(w2q[:, kt, :], 1, ("c8", kt), name=("w2", kt))

        def tables():
            b8_ = [128, NT, 64]
            for j in range(2):
                w = wrow[:, j * 128:(j + 1) * 128]
                tt(DV, tA[:, :, j, :], tA[:, :, j, :], w[:, 0:64].unsqueeze(1).broadcast_to(b8_), ALU.mult,
                   ("table", 0))
                for k in range(2):
                    d_, s_ = slice(32 * k, 32 * k + 32), slice(32 - 32 * k, 64 - 32 * k)
                    tt(DV, tB[:, :, j, d_], tB[:, :, j, d_], w[:, s_].unsqueeze(1).broadcast_to([128, NT, 32]),
                       ALU.mult)
            w = wrow[:, 128:256]
            tt(DV, cA[:, :, :], cA[:, :, :], w[:, 0:64].unsqueeze(1).broadcast_to([128, 2, 64]), ALU.mult)
            for k in range(2):
                d_, s_ = slice(32 * k, 32 * k + 32), slice(32 - 32 * k, 64 - 32 * k)
                tt(DV, cB[:, :, d_], cB[:, :, d_], w[:, s_].unsqueeze(1).broadcast_to([128, 2, 32]), ALU.mult)
            tt(DV, wqk[:, :], wrow[:, 64:128], wrow[:, 192:256], ALU.mult)
            ts(DV, blT[:, :], blT[:, :], 0.5, None, ALU.mult, ALU.bypass, name=("bl", 0))
            qu.at["tab", 0] = qu.at["bl", 0]

        def tile_at(s, lag):
            m = s - lag + 8
            return m // 64 * 8 + m % 64 if 0 <= m < 64 * NB and m % 64 < 8 else None

        def unit(s, lag):
            return s - lag if 0 <= s - lag < NU else None

        qnext = 1
        for s in range(-9, NU + 6):
            U = {lag: unit(s, lag) for lag in range(5)}
            T = {lag: tile_at(s, lag) for lag in range(8)}
            K = {lag: T[lag] // 4 if T[lag] is not None and T[lag] % 4 == 3 else None for lag in range(8)}
            now = [q for q, c in enumerate(chunks) if c[3] == s]

            def do(i, f, *a):
                if i is not None:
                    f(i, *a)

            do(U[4] if U[4] is not None and (U[4] // 8) % 8 == 7 else None, store)
            do(T[5], load_acc)
            while qnext < len(chunks) and chunks[qnext][3] <= s + 1:
                load_chunk(qnext)
                qnext += 1
            if s % 8 == 6 and 0 < s // 8 + 1 < NU // 8:
                load_bias(s // 8 + 1)
            nxt = tile_at(s + 1, 0)
            do(nxt if nxt is not None and nxt >= 2 else None, load_x)

            do(U[1], tr)
            do(U[0], proj_qk)
            do(U[2], turn_p, 0)
            do(T[1], turn_x)
            do(U[1], scores, 0)
            do(U[1], scores, 1)
            do(U[2], turn_p, 1)
            do(K[3], ckv)
            do(K[4], turn_ck)
            do(U[0], proj_v)
            do(T[2], entries)
            do(U[2], values, 0)
            do(T[6], ffn)
            do(U[2], values, 1)
            do(U[3], out_proj)

            do(U[1], hi_qk)
            do(U[2], hi_p, 0)
            for q in now:
                if chunks[q][0] == "o":
                    hi_wo(q)
            do(U[0], evac_qk)
            if T[1] is not None:
                hi_x(T[1])
                cast8(bT[:, :], 0, ("xt", T[1]), *([("q8", T[1] - 1)] if T[1] else [("w2", KT - 1)]),
                      name=("b8", T[1]))
            do(U[0], squares)
            do(U[2], hi_p, 1)
            do(U[1], exps)
            do(T[1], exp_w)
            do(K[3], put_kv)
            do(K[4], hi_ck)
            do(T[2], put_et)
            do(U[0], hi_v)
            do(U[2], hi_c)

            do(U[1], lo_qk)
            do(U[2], pick, 0)
            do(U[2], pick, 1)
            do(U[2], sums)
            do(U[4], add_out)
            for q in now:
                if chunks[q][0] == "o":
                    lo_wo(q)
            do(T[1], normalise)
            do(T[2], weights4)
            do(U[2], lo_p, 0)
            do(U[0], rope_a)
            do(T[1], lo_x)
            do(T[1], group_max)
            do(U[1], top, 0)
            do(U[0], eps_qk)
            do(U[2], lo_p, 1)
            do(U[0], rope_add)
            do(U[1], top, 1)
            do(U[1], neg_max)
            do(U[0], lo_v)
            do(U[0], kscale)
            do(U[2], lo_c)
            if T[1] is not None:
                quant(q8[:, T[1] % QR, :], 0, ("b8", T[1]), ("ff", T[1] - QR), name=("q8", T[1]))
            do(K[3], rope_ck)
            do(K[4], lo_ck)
            do(T[6], init)
            do(T[0], norm_stats)
            if s == -9:
                quant_w2()
                tables()
            if s % 8 == 7 and s // 8 + 1 < NU // 8 and s >= -1:
                bias_rows(s // 8 + 1)
                bias_done(s // 8 + 1)

            do(U[2], normalise_p, 0)
            do(U[2], normalise_p, 1)
            do(U[0], rope_b)
            if U[0] is not None:
                power(r4[:, U[0] % 4], ss[:, U[0] % 4], ("veps", U[0]), name=("r4", U[0]))
            if K[3] is not None:
                power(sm[:, 14:15], sm[:, 13:14], ("cke", K[3]), name=("ckp", K[3]))
            if T[0] is not None:
                power(st[:, 9:10], st[:, 8:9], ("xv", T[0]), ("ones", 0), name=("rstd", T[0]))
            do(T[5], add_bo)
            for q in now:
                if chunks[q][0] == "w":
                    split(q)

        block = ctx.enter_context(nc.Block())

        @block.sync
        def _(e):
            qu.emit("sync", e)

        @block.tensor
        def _(e):
            qu.emit(PE, e)

        @block.scalar
        def _(e):
            qu.emit(AC, e)

        @block.vector
        def _(e):
            qu.emit(DV, e)

        @block.gpsimd
        def _(e):
            qu.emit(PO, e)


def constants():
    import numpy as np

    c = np.zeros((128, C_N), np.float32)
    r = np.arange(128)
    c[:, C_ID:C_ID + 128] = np.eye(128)
    cur = np.where(r[None, :] <= r[:, None], 0.0, NEG)
    prev = np.where(r[None, :] >= r[:, None], 0.0, NEG)
    c[:, C_MK:C_MK + 384] = np.concatenate([cur, prev, cur], 1)
    c[:, C_MG:C_MG + 128] = np.where(r[None, :] // 4 == r[:, None] // 4, 0.0, NEG)
    c[:, C_SEL:C_SEL + 32] = r[:, None] // 4 == np.arange(32)[None, :]
    c[0, C_MR], c[1, C_MR], c[1, C_NR] = 1.0, -1.0, 1.0
    c[:, C_M32:C_M32 + 32] = np.where(4 * np.arange(32)[None, :] + 3 <= r[:, None], 0.0, NEG)
    f = np.float32
    inv = f(1.0) / np.power(f(10000.0), np.arange(32, dtype=f) * f(2.0 / 64))

    def table(pos):
        ang = pos.astype(f)[:, None] * inv[None, :].astype(f)
        co, si = np.cos(ang).astype(f), np.sin(ang).astype(f)
        both = np.stack([np.concatenate([co, co], 1), np.concatenate([-si, si], 1)])
        return np.ascontiguousarray(both.reshape(2, -1, 128, 64).transpose(0, 2, 1, 3))

    return c, table(np.arange(SEQ)), table(np.arange(1, SEQ // 4 + 1) * 4 - 1)


_INS = ["hidden_states", "Wq", "bq", "Wcmp", "bcmp", "Wk", "bk", "Wv", "bv", "Wlk", "blk", "Wlv", "blv",
        "qn_w", "kn_w", "Wo", "bo"]


def kernel(**inputs):
    import numpy as _np
    import concourse.bacc as _bacc
    from concourse.bass_utils import run_bass_kernel_spmd as _run

    nc = _bacc.Bacc("TRN2", target_bir_lowering=False, num_devices=1, dynamic_dma_scratch_size=1024)
    given = {n: inputs["L0_attn_" + n] for n in _INS}
    for n in ("input2", "scale", "scale1"):
        given[n] = inputs["L0_ffn_" + n]
    given["consts"], given["tabs"], given["ctabs"] = constants()
    arrays, args = {}, []
    for name, v in given.items():
        a = _np.ascontiguousarray(v)
        a = a.reshape(1) if a.ndim == 0 else a
        arrays["in_" + name] = a
        args.append(nc.dram_tensor("in_" + name, a.shape, mybir.dt.from_np(a.dtype), kind="ExternalInput").ap())
    out = nc.dram_tensor("out_0", (NB, SEQ, HID), F32, kind="ExternalOutput").ap()
    build(nc, *args, out)
    r = _run(nc, [arrays], core_ids=[0])
    return r.results[0]["out_0"]
```

```python
from contextlib import ExitStack

import concourse.bass as bass
from concourse import mybir

F32 = mybir.dt.float32
F32R = mybir.dt.float32r
BF16 = mybir.dt.bfloat16
F8 = mybir.dt.float8e4
ALU = mybir.AluOpType
ACT = mybir.ActivationFunctionType
AX_X = mybir.AxisListType.X

NB, SEQ, HID, NH, D = 4, 1024, 512, 16, 128
NT = SEQ // 128
KT = HID // 128
NG = NH // 2
NU = NB * NG * NT
NTT = NB * NT
NEG = -1e30
GONE = -3e38
BIG = 3.4e38
RMS_EPS = 128 * 1e-6
SQD = float(D) ** 0.5
XR, QR = 2, 6

C_ID, C_MK, C_MG, C_SEL, C_MR, C_NR, C_M32, C_N = 0, 128, 512, 640, 672, 673, 674, 706


STORE_LAG = 4

ORDER = {
    "tensor": [
        ("scores", 2, 1), ("turn_p", 3, 1), ("ckv", 3), ("proj_qk", 0, 0), ("ffn", 7), ("turn_ck", 5), ("proj_v", 1),
        ("out_proj", 4, 0), ("tr", 1), ("out_proj", 4, 1), ("proj_qk", 0, 1), ("values", 3, 0), ("scores", 1, 0),
        ("values", 3, 1), ("entries", 2), ("turn_x", 1), ("turn_p", 2, 0),
    ],
    "scalar": [
        ("squares", 1), ("evac_qk", 1), ("hi_x", 2), ("hi_c", 4), ("put_et", 3), ("cast_x", 2), ("hi_p", 3, 0),
        ("exp_w", 2), ("exp_l", 2, 0), ("put_kv", 3), ("exp_s", 2, 0), ("hi_p", 3, 1), ("hi_ck", 5), ("exp_s", 2, 1),
        ("kscale", 1), ("exp_l", 2, 1), ("hi_v", 1), ("hi_qk", 1), ("hi_wo", 5),
    ],
    "vector": [
        ("max8", 2, 0), ("mask_max", 2, 0), ("eps_qk", 1), ("group_max", 2), ("neg_max", 2, 0), ("strike", 2, 0),
        ("rope_a", 1), ("lo_c", 4), ("max8", 2, 1), ("mask_max", 2, 1), ("rope_ck", 5), ("rope_rest", 1),
        ("neg_max", 2, 1), ("strike", 2, 1), ("norm_stats", 1), ("rope_add", 1), ("lo_x", 2), ("init", 7),
        ("lo_p", 3, 0), ("lo_ck", 5), ("pick", 2, 0), ("pick", 2, 1), ("weights4", 2), ("sums", 2), ("neg_r", 1),
        ("lo_p", 3, 1), ("inverse", 2), ("lo_v", 1), ("lo_qk", 1), ("add_out", 4), ("lo_wo", 0), ("normalise", 1),
        ("quant_x", 2),
    ],
    "gpsimd": [
        ("add_bo", 7), ("normalise_p", 3, 0), ("normalise_p", 3, 1), ("rope_b", 1), ("power_ck", 5), ("power_qk", 1),
        ("split", 5), ("power_x", 1),
    ],
}


class Queues:

    def __init__(self, sem):
        self.sem, self.ops, self.n, self.at = sem, {}, {}, {}

    def put(self, eng, fn, *waits, name=None, quiet=False):
        self.ops.setdefault(eng, []).append((fn, waits, None if quiet else eng, 1))
        if not quiet:
            self.n[eng] = self.n.get(eng, 0) + 1
        if name is not None:
            assert not quiet and name not in self.at, name
            self.at[name] = (eng, self.n[eng])

    def dma(self, fn, stream, *waits, name=None):
        self.ops.setdefault("sync", []).append((fn, waits, stream, 16))
        self.n[stream] = self.n.get(stream, 0) + 16
        if name is not None:
            self.at[name] = (stream, self.n[stream])

    def emit(self, eng, e):
        seen = {}
        for fn, waits, on, v in self.ops.get(eng, []):
            need = {}
            for w in waits:
                if not isinstance(w[1], int) or w[1] >= 0:
                    s, c = self.at[w]
                    need[s] = max(need.get(s, 0), c)
            for s, c in need.items():
                if seen.get(s, 0) < c:
                    e.wait_ge(self.sem(s), c)
                    seen[s] = c
            i = fn(e)
            if on is not None:
                i.then_inc(self.sem(on), v)
        for s in sorted(k for k in self.n if k.startswith("d_")) if eng == "sync" else []:
            e.wait_ge(self.sem(s), self.n[s])


def build(nc, x, Wq, bq, Wcmp, bcmp, Wk, bk, Wv, bv, Wlk, blk, Wlv, blv, qnw, knw, Wo, bo,
          W2, sc0, sc1, consts, tabs, ctabs, out):
    ctx = ExitStack()
    S = {}

    def sb(name, shape, dt=F32):
        return ctx.enter_context(nc.sbuf_tensor(name, shape, dt))

    def ps(name, shape):
        return ctx.enter_context(nc.psum_tensor(name, shape, F32))

    def sem(name):
        if name not in S:
            S[name] = ctx.enter_context(nc.semaphore("s_" + name))
        return S[name]

    with ctx:
        xh = sb("xh", [128, KT, SEQ], F32R)
        xl = sb("xl", [128, KT, SEQ], F32R)
        wr = sb("wr", [128, 2, 512])
        wh = sb("wh", [128, 2, KT, 768], F32R)
        wl = sb("wl", [128, 2, KT, 768], F32R)
        woh = sb("woh", [128, 2, 512], F32R)
        wol = sb("wol", [128, 2, 512], F32R)
        acc = sb("acc", [128, NT, 512])
        qkh = sb("qkh", [128, 3, 2, 2, 128], F32R)
        qkl = sb("qkl", [128, 3, 2, 2, 128], F32R)
        vh = sb("vh", [128, 4, 2, 128], F32R)
        vl = sb("vl", [128, 4, 2, 128], F32R)
        raw = sb("raw", [128, 2, 2, 2, 128])
        t1 = sb("t1", [128, 2, 2, 64])
        t2 = sb("t2", [128, 2, 2, 64])
        tA = sb("tA", [128, NT, 2, 64])
        tB = sb("tB", [128, NT, 2, 64])
        cA = sb("cA", [128, 2, 64])
        cB = sb("cB", [128, 2, 64])
        wqk = sb("wqk", [128, 64])
        P = sb("P", [128, 2, 2, 512])
        es = sb("es", [128, 2, 256])
        rp = sb("rp", [128, 2, 256])
        pth = sb("pth", [128, 2, 512], F32R)
        ptl = sb("ptl", [128, 2, 512], F32R)
        ch = sb("ch", [128, 2, 2, 128], F32R)
        cl = sb("cl", [128, 2, 2, 128], F32R)
        ckh = sb("ckh", [128, 2, 256], F32R)
        ckl = sb("ckl", [128, 2, 256], F32R)
        cvh = sb("cvh", [128, 2, 2, 128], F32R)
        cvl = sb("cvl", [128, 2, 2, 128], F32R)
        xt = sb("xt", [128, XR, 512])
        q8 = sb("q8", [128, QR, 512], BF16)
        a8 = sb("a8", [128, 512], F8)
        b8 = sb("b8", [128, 512], F8)
        qa = sb("qa", [128, 512], BF16)
        qb = sb("qb", [128, 512], BF16)
        w2q = sb("w2q", [128, KT, 512], BF16)
        et = sb("et", [128, KT, 128])
        wkv = sb("wkv", [128, KT, 256])
        bkv = sb("bkv", [1, 256])
        ckr = sb("ckr", [128, 256])
        ct = sb("ct", [128, 2, 64])
        wcb = sb("wcb", [128, 512])
        bob = sb("bob", [128, 512])
        br = sb("br", [128, 2, 2, 128])
        bh = sb("bh", [128, 2, 512], F32R)
        cst = sb("cst", [128, C_N])
        idb = sb("idb", [128, 128], BF16)
        m32 = sb("m32", [128, 32], BF16)
        onef = sb("onef", [128, 128])
        oner = sb("oner", [128, 128], F32R)
        junk = sb("junk", [128, 5, 128], BF16)
        junkd = sb("junkd", [128, 512], BF16)
        dg = sb("dg", [128, 128])
        eg = sb("eg", [128, 128])
        wm = sb("wm", [128, 32])
        sm = sb("sm", [128, 16])
        st = sb("st", [128, 12])
        mh = sb("mh", [128, 4])
        ss = sb("ss", [128, 4, 4])
        r4 = sb("r4", [128, 4, 4])
        ngr = sb("ngr", [128, 4, 2])
        mm = sb("mm", [128, 4, 2, 9])
        nm = sb("nm", [128, 4, 2, 2])
        su = sb("su", [128, 4, 2, 2])
        rs = sb("rs", [128, 4, 2, 2])
        blT = sb("blT", [128, NH])
        isc = sb("isc", [128, 5])
        bcm = sb("bcm", [128, 1])
        wrow = P[:, 1, 0, 0:256]

        bQK = ps("bQK", [128, 512])
        bVC = ps("bVC", [128, 512])
        bT = ps("bT", [128, 512])
        bS = [ps("bS0", [128, 512]), ps("bS1", [128, 512])]
        bP = [ps("bP0", [128, 512]), ps("bP1", [128, 512])]
        bY = ps("bY", [128, 512])

        ident = cst[:, C_ID:C_ID + 128]

        def flat(ap):
            return ap.rearrange("p a b c -> p (a b c)")

        def f32(ap):
            return ap.bitcast(F32)

        qu = Queues(sem)
        put, dma = qu.put, qu.dma
        PE, AC, DV, PO = "tensor", "scalar", "vector", "gpsimd"

        def slots_of(u):
            s = u % 3
            return [s] if u % 8 == 0 else [0, 2] if s == 0 else [s - 1, s]

        def units_of(u):
            return [u] if u % 8 == 0 else [u, u - 1] if u % 3 == 0 else [u - 1, u]

        def mask_of(u):
            a = C_MK + (0 if u % 3 == 0 or u % 8 == 0 else 128)
            return cst[:, a:a + nloc(u)]

        def width(u):
            return 32 * (u % 8 + 1)

        def nloc(u):
            return 128 if u % 8 == 0 else 256

        def pblocks(u):
            return ([0] if u % 8 == 0 else [0, 1]) + ([2] if u % 8 < 4 else [2, 3])

        chunks = []
        for s in range(-8, NU):
            gi, i = s // 8, s % 8
            if i == 3 and gi >= 0:
                chunks += [("o", gi, 0, s), ("o", gi, 1, s)]
            if i != 3 and i != 7 and gi + 1 < NU // 8:
                chunks.append(("w", gi + 1, i if i < 3 else i - 1, s))
        where = {(k, gi, c): q for q, (k, gi, c, _) in enumerate(chunks)}

        def load_x(t):
            dma(lambda e: e.dma_start(xt[:, t % XR, :], x[t // 8, (t % 8) * 128:(t % 8 + 1) * 128, :]),
                f"d_x{t % XR}", ("et", t - XR), name=("x", t))

        def load_chunk(q):
            k, gi, c, _ = chunks[q]
            g = gi % NG
            free = [("wohi", q - 2), ("wolo", q - 2)] if q >= 2 and chunks[q - 2][0] == "o" else [("split", q - 2)]
            dst, stream = wr[:, q % 2, :], f"d_w{q % 2}"
            if k == "o":
                h = 2 * g + c
                dma(lambda e: e.dma_start(dst, Wo[h * 128:(h + 1) * 128, :]), stream, *free, name=("w", q))
            elif c < 4:
                d4 = dst.rearrange("p (h k d) -> p h k d", h=2, k=2)
                for j, w in enumerate((Wq, Wlk)):
                    src = w[c * 128:(c + 1) * 128, g * 256:(g + 1) * 256].rearrange("p (h d) -> p h d", h=2)
                    dma(lambda e, j=j, src=src: e.dma_start(d4[:, :, j, :], src), stream, *free,
                        name=("w", q) if j else None)
            else:
                k0 = 2 * (c - 4)
                src = Wlv[k0 * 128:(k0 + 2) * 128, g * 256:(g + 1) * 256].rearrange("(k p) n -> p k n", p=128)
                dma(lambda e: e.dma_start(dst.rearrange("p (k n) -> p k n", k=2), src), stream, *free,
                    name=("w", q))

        def load_bias(gi):
            g = gi % NG
            for j, w in enumerate((bq, blk)):
                for h in range(2):
                    o = g * 256 + h * 128
                    src = w[o:o + 128].rearrange("(a d) -> a d", a=1).broadcast_to([128, 128])
                    dma(lambda e, h=h, j=j, src=src: e.dma_start(br[:, h, j, :], src), "d_b", ("bias", gi - 1),
                        name=("br", gi) if h + j == 2 else None)

        def bc(ap, n):
            return ap.rearrange("(a n) -> a n", a=1).broadcast_to([128, n])

        def first_loads():
            def load(stream, dst, src, name=None, **kw):
                dma(lambda e: e.dma_start(dst, src, **kw), stream, name=name)

            load("d_c", cst[:, :], consts)
            load("d_c", wcb[:, :], Wcmp.rearrange("n a -> a n").broadcast_to([128, 512]))
            load("d_c", bcm[:, :], bc(bcmp, 1))
            load("d_c", isc[:, 0:1], bc(sc0, 1))
            load("d_c", isc[:, 1:2], bc(sc1, 1), name=("const", 0))
            load_x(0)
            load("d_2", acc[:, 0:KT, :], W2.rearrange("(k p) n -> p k n", p=128), name=("w2raw", 0))
            load_chunk(0)
            load_x(1)
            load("d_t", wrow[:, 0:128], bc(qnw, 128))
            load("d_t", wrow[:, 128:256], bc(knw, 128))
            for j in range(2):
                load("d_t", tA[:, :, j, :], tabs[0])
                load("d_t", tB[:, :, j, :], tabs[1])
            load("d_t", cA[:, :, :], ctabs[0])
            load("d_t", cB[:, :, :], ctabs[1])
            load("d_t", wkv[:, :, 0:128], Wk.rearrange("(k p) n -> p k n", p=128))
            load("d_t", wkv[:, :, 128:256], Wv.rearrange("(k p) n -> p k n", p=128))
            load("d_t", bkv[:, 0:128], bk.rearrange("(a n) -> a n", a=1))
            load("d_t", bkv[:, 128:256], bv.rearrange("(a n) -> a n", a=1))
            load("d_t", bob[:, :], bc(bo, 512))
            load("d_t", blT[:, :], blv.rearrange("(h d) -> d h", d=128), name=("table", 0),
                 allow_slow_non_contiguous=True)
            load_bias(0)

        def load_acc(t):
            wait = [("store", t - 8)] if t >= 8 else [("w2", KT - 1), ("blvo", 3)]
            dma(lambda e: e.dma_start(acc[:, t % 8, :], x[t // 8, (t % 8) * 128:(t % 8 + 1) * 128, :]),
                f"d_a{t % 8}", *wait, name=("xacc", t))

        def store(u):
            b, i = u // 64, u % 8
            dma(lambda e: e.dma_start(out[b, i * 128:(i + 1) * 128, :], acc[:, i, :]), f"d_o{i}", ("acc", u),
                name=("store", b * 8 + i))

        free = {"T": [], "Y": [], "V": []}

        def mm_(dst, a, b, start, stop, *waits, name=None):
            put(PE, lambda e: e.matmul(dst, a, b, start=start, stop=stop), *waits, name=name, quiet=name is None)

        def turn_(dst, src, *waits, name=None):
            put(PE, lambda e: e.transpose(dst, src, ident), *waits, name=name, quiet=name is None)

        def three(dst, ah, al, bh_, bl_, first, last, *waits, name=None):
            mm_(dst, ah, bh_, first, False, *waits)
            mm_(dst, ah, bl_, False, False)
            mm_(dst, al, bh_, False, last, name=name)

        def tr(u):
            for k in range(4):
                turn_(bT[:, k * 128:(k + 1) * 128], raw[:, u % 2, k // 2, k % 2, :], ("kscale", u), ("add", u), ("const", 0),
                      *free["T"], name=("tr", u) if k == 3 else None)
            free["T"] = [("hi_qk", u), ("lo_qk", u)]

        def proj_qk(u, half):
            gi, i, w = u // 8, u % 8, u // 8 % 2
            waits = [("raw", u - 1), ("sq", u - 1), ("split", where["w", gi, 3]), ("bias", gi)]
            if gi % NG == 0:
                waits += [("hi_x", u // 64 * 8 + i), ("lo_x", u // 64 * 8 + i)]
            c = slice(i * 128, (i + 1) * 128)
            for kt in (0, 1) if half == 0 else (2, 3):
                three(bQK[:, :], xh[:, kt, c], xl[:, kt, c], wh[:, w, kt, 0:512], wl[:, w, kt, 0:512],
                      kt == 0, False, *waits)
            if half:
                mm_(bQK[:, :], oner[:, :], bh[:, w, :], False, True, name=("qk", u))

        def proj_v(u):
            gi, i, w = u // 8, u % 8, u // 8 % 2
            waits = [*free["V"], ("split", where["w", gi, 5])]
            if gi % NG == 0:
                waits += [("hi_x", u // 64 * 8 + i), ("lo_x", u // 64 * 8 + i)]
            free["V"] = [("hi_v", u), ("lo_v", u)]
            c = slice(i * 128, (i + 1) * 128)
            for kt in range(KT):
                three(bVC[:, 0:256], xh[:, kt, c], xl[:, kt, c], wh[:, w, kt, 512:768], wl[:, w, kt, 512:768],
                      kt == 0, kt == KT - 1, *waits, name=("v", u) if kt == KT - 1 else None)

        def scores(u, h):
            b, i, C = u // 64, u % 8, width(u)
            k = 2 * b + i // 4
            waits = [("hi_qk", u), ("lo_qk", u), ("hi_ck", k), ("lo_ck", k), ("mr", 2 * (u - 1) + h),
                     ("es", 2 * (u - 1) + h)]
            sl = slots_of(u)
            keys = slice(sl[0], sl[-1] + 1, max(sl[-1] - sl[0], 1))
            q_, ql_ = qkh[:, u % 3, h, 0, :], qkl[:, u % 3, h, 0, :]
            three(bS[h][:, 0:nloc(u)], q_, ql_, qkh[:, keys, h, 1, :], qkl[:, keys, h, 1, :], True, True, *waits)
            cmp = bS[h][:, 256:256 + C]
            mm_(cmp, q_, ckh[:, b % 2, 0:C], True, False)
            mm_(cmp, q_, ckl[:, b % 2, 0:C], False, False)
            mm_(bS[h][:, 256 + C - 32:256 + C], idb[:, :], m32[:, :], False, False)
            mm_(cmp, ql_, ckh[:, b % 2, 0:C], False, True, name=("s", 2 * u + h))

        def turn_p(u, h):
            a = 2 * u + h
            bl = pblocks(u)
            for n, k in enumerate(bl):
                turn_(bP[h][:, n * 128:(n + 1) * 128], P[:, u % 2, h, k * 128:(k + 1) * 128], ("norm", a),
                      ("hi_p", a - 2), ("lo_p", a - 2), name=("pt", a) if n == len(bl) - 1 else None)

        def values(u, h):
            a, b, i = 2 * u + h, u // 64, u % 8
            k = 2 * b + i // 4
            waits = [("hi_p", a), ("lo_p", a), ("hi_v", u), ("lo_v", u), ("hi_cv", k), ("lo_cv", k),
                     *free["V"]]
            if h:
                free["V"] = [("hi_c", u), ("lo_c", u)]
            vals = [(vh[:, t % 4, h, :], vl[:, t % 4, h, :]) for t in units_of(u)]
            vals += [(cvh[:, b % 2, n, :], cvl[:, b % 2, n, :]) for n in range(i // 4 + 1)]
            for n, (v_, vl_) in enumerate(vals):
                c = slice(n * 128, (n + 1) * 128)
                last = n == len(vals) - 1
                three(bVC[:, 256 + h * 128:384 + h * 128], v_, vl_, pth[:, h, c], ptl[:, h, c], n == 0, last,
                      *waits, name=("c", a) if last else None)

        def out_proj(u, h):
            gi = u // 8
            waits = [("hi_c", u), ("lo_c", u), ("wolo", where["o", gi, 1]), ("wohi", where["o", gi, 1])]
            three(bY[:, :], ch[:, u % 2, h, :], cl[:, u % 2, h, :], woh[:, h, :], wol[:, h, :], h == 0, h == 1,
                  *waits, *(free["Y"] if h == 0 else ()), name=("wo", u) if h else None)
            free["Y"] = [("acc", u)]

        def turn_x(t):
            for kt in range(KT):
                turn_(bT[:, kt * 128:(kt + 1) * 128], xt[:, t % XR, kt * 128:(kt + 1) * 128], ("xn", t),
                      *free["T"], name=("xt", t) if kt == KT - 1 else None)
            free["T"] = [("hi_x", t), ("b8", t), ("lo_x", t)]
            mm_(bY[:, 0:128], onef[:, :], dg[:, :], True, True, ("dg", t), *free["Y"], name=("bc", t))
            free["Y"] = [("eg", t)]

        def entries(t):
            for kt in range(KT):
                mm_(bY[:, kt * 32:(kt + 1) * 32], xt[:, t % XR, kt * 128:(kt + 1) * 128], wm[:, :], True, True,
                    ("wm", t), *free["Y"], name=("et", t) if kt == KT - 1 else None)
            free["Y"] = [("put_et", t)]

        def ckv(k):
            for kt in range(KT):
                mm_(bY[:, 0:256], et[:, kt, :], wkv[:, kt, :], kt == 0, False, ("put_et", 4 * k + 3), *free["Y"])
            mm_(bY[:, 0:256], onef[0:1, :], bkv[:, :], False, True, name=("kv", k))
            free["Y"] = [("css", k)]

        def turn_ck(k):
            turn_(bT[:, 0:128], ckr[:, 0:128], ("cks", k), *free["T"], name=("ct", k))
            free["T"] = [("hi_ck", k), ("lo_ck", k)]

        def ffn(t):
            for kt in range(KT):
                mm_(bY[:, :], q8[:, t % QR, kt * 128:(kt + 1) * 128], w2q[:, kt, :], kt == 0, kt == KT - 1,
                    ("q8", t), *free["Y"], name=("ff", t) if kt == KT - 1 else None)
            free["Y"] = [("init", t)]

        def act(dst, src, func, *waits, name=None, **kw):
            put(AC, lambda e: e.activation(dst, src, func, **kw), *waits, name=name)

        def hi_qk(u):
            act(flat(qkh[:, u % 3]), bT[:, :], ACT.Copy, ("tr", u), ("s", 2 * (u - 2)), ("s", 2 * (u - 2) + 1),
                ("lo_qk", u - 3),
                name=("hi_qk", u))

        def hi_p(u, h):
            n = len(pblocks(u)) * 128
            act(pth[:, h, 0:n], bP[h][:, 0:n], ACT.Copy, ("pt", 2 * u + h), ("c", 2 * (u - 1) + h),
                name=("hi_p", 2 * u + h))

        def evac_qk(u):
            act(flat(raw[:, u % 2]), bQK[:, :], ACT.Copy, ("qk", u), ("tr", u - 2), name=("raw", u))

        def squares(u):
            for k in range(4):
                act(junk[:, k, :], bQK[:, k * 128:(k + 1) * 128], ACT.Square, ("qk", u), ("sq", u - 1),
                    accum_out=ss[:, u % 4, k:k + 1], name=("sq", u) if k == 3 else None)

        def kscale(u):
            for h in range(2):
                k_ = raw[:, u % 2, h, 1, :]
                act(k_, k_, ACT.Copy, ("r4", u), ("add", u), ("krest", u), scale=r4[:, u % 4, 2 * h + 1:2 * h + 2],
                    name=("kscale", u) if h else None)

        def exp_l(u, h):
            pl = P[:, u % 2, h, 0:nloc(u)]
            act(pl, pl, ACT.Exp, ("nm", 2 * u + h), scale=r4[:, u % 4, 2 * h:2 * h + 1], bias=nm[:, u % 4, h, 1:2],
                accum_out=su[:, u % 4, h, 1:2], name=("el", 2 * u + h))

        def exp_s(u, h):
            C = width(u)
            act(es[:, h, 0:C], bS[h][:, 256:256 + C], ACT.Exp, ("nm", 2 * u + h), ("mr", 2 * u + h),
                ("stt", 2 * (u - 1) + h),
                scale=r4[:, u % 4, 2 * h:2 * h + 1], bias=nm[:, u % 4, h, 0:1], name=("es", 2 * u + h))

        def hi_v(u):
            act(vh[:, u % 4].rearrange("p a b -> p (a b)"), bVC[:, 0:256], ACT.Copy, ("v", u),
                ("c", 2 * (u - 3)), ("c", 2 * (u - 3) + 1), name=("hi_v", u))

        def hi_c(u):
            act(ch[:, u % 2].rearrange("p a b -> p (a b)"), bVC[:, 256:512], ACT.Copy, ("c", 2 * u), ("c", 2 * u + 1),
                ("wo", u - 2), name=("hi_c", u))

        def hi_wo(q):
            gi, c = chunks[q][1:3]
            act(woh[:, c, :], wr[:, q % 2, :], ACT.Copy, ("w", q), ("wo", 8 * gi - 1), name=("wohi", q))

        def hi_x(t):
            b, j = t // 8, t % 8
            src = bT[:, :].rearrange("p (k c) -> p k c", k=KT)
            act(xh[:, :, j * 128:(j + 1) * 128], src, ACT.Copy, ("xt", t),
                ("qk", (b - 1) * 64 + 56 + j), ("v", (b - 1) * 64 + 56 + j),
                name=("hi_x", t))

        def cast8(src, i, *waits, name):
            act(a8[:, :], src, ACT.Copy, *waits, scale=isc[:, i:i + 1], saturate=False)
            act(b8[:, :], src, ACT.Copy, scale=isc[:, i + 2:i + 3], saturate=False, name=name)

        def cast_x(t):
            cast8(bT[:, :], 0, ("xt", t), *([("q8", t - 1)] if t else [("w2", KT - 1)]), name=("b8", t))

        def exp_w(t):
            act(eg[:, :], eg[:, :], ACT.Exp, ("neg", t), ("wtok", t - 1), bias=sm[:, 3:4], accum_out=sm[:, 4:5])
            act(sm[:, 5:6], sm[:, 2:3], ACT.Exp, bias=sm[:, 3:4], name=("ew", t))

        def put_et(t):
            act(et[:, :, (t % 4) * 32:(t % 4 + 1) * 32], bY[:, 0:128].rearrange("p (k c) -> p k c", k=KT),
                ACT.Copy, ("et", t), ("kv", t // 4 - 1), name=("put_et", t))

        def put_kv(k):
            b = k // 2
            act(ckr[:, :], bY[:, 0:256], ACT.Copy, ("kv", k), ("ct", k - 1), ("lo_cv", k - 1), name=("kvr", k))
            act(cvh[:, b % 2, k % 2, :], bY[:, 128:256], ACT.Copy, ("c", 2 * (64 * (b - 1) - 1) + 1),
                name=("hi_cv", k))
            act(junk[:, 4, :], bY[:, 0:128], ACT.Square, ("css", k - 1), accum_out=sm[:, 12:13], name=("css", k))

        def hi_ck(k):
            b = k // 2
            act(ckh[:, b % 2, (k % 2) * 128:(k % 2 + 1) * 128], bT[:, 0:128], ACT.Copy, ("ct", k),
                ("s", 2 * (64 * (b - 1) - 1) + 1), name=("hi_ck", k))

        def tt(eng, dst, a, b, op, *waits, name=None):
            put(eng, lambda e: e.tensor_tensor(dst, a, b, op), *waits, name=name)

        def ts(eng, dst, a, s1, s2, op0, op1, *waits, name=None, **kw):
            put(eng, lambda e: e.tensor_scalar(dst, a, s1, s2, op0, op1, **kw), *waits, name=name)

        def stt(dst, a, s, b, op0, op1, *waits, name=None, **kw):
            put(DV, lambda e: e.scalar_tensor_tensor(out=dst, in0=a, scalar=s, in1=b, op0=op0, op1=op1, **kw),
                *waits, name=name)

        def lo(dst, src, hi, *waits, name):
            tt(DV, dst, src, f32(hi), ALU.subtract, *waits, name=name)

        def lo_qk(u):
            lo(flat(qkl[:, u % 3]), bT[:, :], flat(qkh[:, u % 3]), ("hi_qk", u), ("lo_qk", u - 1), name=("lo_qk", u))

        def pick(u, h):
            C = width(u)
            stt(P[:, u % 2, h, 256:256 + C], rp[:, h, 0:C], GONE, es[:, h, 0:C], ALU.is_equal, ALU.mult,
                ("es", 2 * u + h), ("mr", 2 * u + h), ("pt", 2 * (u - 2) + h), accum_out=su[:, u % 4, h, 0:1],
                name=("stt", 2 * u + h))

        def sums(u):
            if u % 8:
                return
            ts(DV, rs[:, u % 4], su[:, u % 4], 1e-9, None, ALU.max, ALU.bypass, ("stt", 2 * u), ("stt", 2 * u + 1),
               ("el", 2 * u), ("el", 2 * u + 1), name=("rs0", u))

        def inverse(u):
            put(DV, lambda e: e.reciprocal(rs[:, u % 4], (su if u % 8 else rs)[:, u % 4]), ("stt", 2 * u),
                ("stt", 2 * u + 1), ("el", 2 * u), ("el", 2 * u + 1), *([] if u % 8 else [("rs0", u)]), name=("rs", u))

        def lo_p(u, h):
            n = len(pblocks(u)) * 128
            a = 2 * u + h
            lo(ptl[:, h, 0:n], bP[h][:, 0:n], pth[:, h, 0:n], ("hi_p", a), ("lo_p", a - 2), name=("lo_p", a))

        def rope_a(u):
            b_ = [128, 2, 2, 64]
            tt(DV, t1[:, :, :, :], raw[:, u % 2, :, :, 0:64], tA[:, u % 8].unsqueeze(1).broadcast_to(b_), ALU.mult,
               ("raw", u), ("tab", 0), ("add", u - 1), name=("t1", u))

        def rope_rest(u):
            kr = raw[:, u % 2, :, 1, 64:128]
            tt(DV, kr, kr, wqk[:, :].unsqueeze(1).broadcast_to([128, 2, 64]), ALU.mult, ("raw", u), ("tab", 0),
               name=("krest", u))

        def eps_qk(u):
            ts(DV, ss[:, u % 4], ss[:, u % 4], RMS_EPS, None, ALU.add, ALU.bypass, ("sq", u), name=("veps", u))

        def rope_add(u):
            tt(DV, raw[:, u % 2, :, :, 0:64], t1[:, :, :, :], t2[:, :, :, :], ALU.add, ("t1", u), ("t2", u),
               name=("add", u))

        def neg_r(u):
            if u % 8:
                return
            ts(DV, ngr[:, u % 4], r4[:, u % 4, 0:4:2], -1.0, None, ALU.mult, ALU.bypass, ("r4", u), name=("ngr", u))

        def max8(u, h):
            put(DV, lambda e: e.max(mm[:, u % 4, h, 0:8], bS[h][:, 256:256 + width(u)]), ("s", 2 * u + h),
                name=("m8", 2 * u + h))

        def mask_max(u, h):
            put(DV, lambda e: e.tensor_tensor_reduce(P[:, u % 2, h, 0:nloc(u)], bS[h][:, 0:nloc(u)], mask_of(u), 1.0,
                                                     GONE, ALU.add, ALU.max, mm[:, u % 4, h, 8:9]),
                ("s", 2 * u + h), ("pt", 2 * (u - 2) + h), name=("ttr", 2 * u + h))

        def strike(u, h):
            C, a = width(u), 2 * u + h
            put(DV, lambda e: e.match_replace(rp[:, h, 0:C], mm[:, u % 4, h, 0:8], bS[h][:, 256:256 + C], GONE),
                ("m8", a), ("ttr", a), ("stt", a - 2), name=("mr", a))

        def neg_max(u, h):
            m = mm[:, u % 4, h, 0:9:8]
            if u % 8 == 0:
                r_, s_, op, after = ngr[:, u % 4, h:h + 1], NEG / 10, ALU.max, ("ngr", u)
            else:
                r_, s_, op, after = r4[:, u % 4, 2 * h:2 * h + 1], -1.0, ALU.mult, ("r4", u)
            ts(DV, nm[:, u % 4, h], m, s_, r_, op, ALU.mult, ("m8", 2 * u + h), ("ttr", 2 * u + h), after,
               name=("nm", 2 * u + h))

        def lo_v(u):
            fl_ = lambda a: a[:, u % 4].rearrange("p a b -> p (a b)")
            lo(fl_(vl), bVC[:, 0:256], fl_(vh), ("hi_v", u), ("lo_v", u - 1), name=("lo_v", u))

        def lo_c(u):
            fl_ = lambda a: a[:, u % 2].rearrange("p a b -> p (a b)")
            lo(fl_(cl), bVC[:, 256:512], fl_(ch), ("hi_c", u), ("lo_c", u - 1), name=("lo_c", u))

        def add_out(u):
            a = acc[:, u % 8, :]
            first = [("init", u // 64 * 8 + u % 8)] if (u // 8) % 8 == 0 else [("acc", u - 8)]
            tt(DV, a, bY[:, :], a, ALU.add, ("wo", u), *first, name=("acc", u))

        def lo_wo(q):
            c = chunks[q][2]
            lo(wol[:, c, :], wr[:, q % 2, :], woh[:, c, :], ("wohi", q), name=("wolo", q))

        def norm_stats(t):
            xs = xt[:, t % XR, :]
            put(DV, lambda e: e.bn_stats(st[:, 0:6], xs), ("x", t), ("xn", t - 1), name=("bs", t))
            put(DV, lambda e: e.bn_aggr(st[:, 6:8], st[:, 0:6]), ("bs", t), name=("ba", t))
            ts(DV, st[:, 8:9], st[:, 7:8], 1e-5, None, ALU.add, ALU.bypass, ("ba", t), ("rstd", t - 1), name=("xv", t))

        def normalise(t):
            xs = xt[:, t % XR, :]
            ts(DV, xs, xs, st[:, 6:7], st[:, 9:10], ALU.subtract, ALU.mult, ("rstd", t), ("ba", t), name=("xn", t))
            put(DV, lambda e: e.tensor_tensor_reduce(junkd[:, :], xs, wcb[:, :], 1.0, 0.0, ALU.mult, ALU.add,
                                                     sm[:, 0:1]), ("xn", t), ("wl", t - 1), name=("wl", t))
            ts(DV, sm[:, 2:3], sm[:, 0:1], bcm[:, 0:1], None, ALU.add, ALU.bypass, ("wl", t), ("ew", t - 1),
               name=("wlb", t))
            ts(DV, dg[:, :], ident, sm[:, 2:3], None, ALU.mult, ALU.bypass, ("wlb", t), ("bc", t - 1),
               name=("dg", t))

        def lo_x(t):
            j = t % 8
            c = slice(j * 128, (j + 1) * 128)
            lo(xl[:, :, c], bT[:, :].rearrange("p (k c) -> p k c", k=KT), xh[:, :, c], ("hi_x", t),
               ("b8", t), name=("lo_x", t))

        def group_max(t):
            put(DV, lambda e: e.tensor_tensor_reduce(eg[:, :], bY[:, 0:128], cst[:, C_MG:C_MG + 128], 1.0, GONE,
                                                     ALU.add, ALU.max, sm[:, 9:10]),
                ("bc", t), ("ew", t - 1), name=("eg", t))
            ts(DV, sm[:, 3:4], sm[:, 9:10], -1.0, None, ALU.mult, ALU.bypass, ("eg", t), name=("neg", t))

        def quant(dst, i, *waits, name):
            ts(DV, qa[:, :], a8[:, :], 240.0, -240.0, ALU.min, ALU.max, *waits)
            ts(DV, qb[:, :], b8[:, :], 120.0, -120.0, ALU.min, ALU.max, name=("qb", name))
            tt(DV, qb[:, :], b8[:, :], qb[:, :], ALU.subtract, ("qb", name), name=("qd", name))
            stt(dst, qb[:, :], 2.0, qa[:, :], ALU.mult, ALU.add, ("qd", name), name=("qs", name))
            ts(DV, qb[:, :], dst, BIG / 450.0, 0.0, ALU.mult, ALU.mult, ("qs", name), name=("qn", name))
            tt(DV, dst, dst, qb[:, :], ALU.add, ("qn", name), name=name)

        def quant_x(t):
            quant(q8[:, t % QR, :], 0, ("b8", t), ("ff", t - QR), name=("q8", t))

        def weights4(t):
            put(DV, lambda e: e.reciprocal(sm[:, 10:11], sm[:, 4:5]), ("ew", t), name=("re", t))
            tt(DV, sm[:, 11:12], sm[:, 10:11], sm[:, 5:6], ALU.mult, ("re", t), name=("wtok", t))
            ts(DV, wm[:, :], cst[:, C_SEL:C_SEL + 32], sm[:, 11:12], None, ALU.mult, ALU.bypass, ("wtok", t),
               ("et", t - 1), name=("wm", t))

        def init(t):
            a = acc[:, t % 8, :]
            stt(a, bY[:, :], isc[:, 4:5], a, ALU.mult, ALU.add, ("ff", t), ("bo", t), ("isc", 0), name=("init", t))

        def rope_ck(k):
            ts(DV, sm[:, 13:14], sm[:, 12:13], RMS_EPS, None, ALU.add, ALU.bypass, ("css", k), name=("cke", k))
            tt(DV, ct[:, 0, :], ckr[:, 0:64], cA[:, k % 2, :], ALU.mult, ("kvr", k), ("tab", 0), ("cadd", k - 1))
            tt(DV, ct[:, 1, 0:32], ckr[:, 32:64], cB[:, k % 2, 0:32], ALU.mult)
            tt(DV, ct[:, 1, 32:64], ckr[:, 0:32], cB[:, k % 2, 32:64], ALU.mult, name=("cm", k))
            tt(DV, ckr[:, 64:128], ckr[:, 64:128], wqk[:, :], ALU.mult, name=("crest", k))
            tt(DV, ckr[:, 0:64], ct[:, 0, :], ct[:, 1, :], ALU.add, ("cm", k), name=("cadd", k))
            ts(DV, ckr[:, 0:128], ckr[:, 0:128], sm[:, 14:15], None, ALU.mult, ALU.bypass, ("ckp", k), ("cadd", k),
               ("crest", k), name=("cks", k))
            lo(cvl[:, (k // 2) % 2, k % 2, :], ckr[:, 128:256], cvh[:, (k // 2) % 2, k % 2, :], ("hi_cv", k),
               name=("lo_cv", k))

        def lo_ck(k):
            b, c = k // 2, slice((k % 2) * 128, (k % 2 + 1) * 128)
            lo(ckl[:, b % 2, c], bT[:, 0:128], ckh[:, b % 2, c], ("hi_ck", k), name=("lo_ck", k))

        def power(dst, src, *waits, name):
            tt(PO, dst, src, mh[:, 0:src.shape[1]], ALU.pow, *waits, name=name)

        def power_qk(u):
            v = 2 * (u - 4)
            power(r4[:, u % 4], ss[:, u % 4], ("veps", u), ("kscale", u - 4), ("el", v), ("el", v + 1), ("es", v),
                  ("es", v + 1), name=("r4", u))

        def power_x(t):
            power(st[:, 9:10], st[:, 8:9], ("xv", t), ("ones", 0), name=("rstd", t))

        def power_ck(k):
            power(sm[:, 14:15], sm[:, 13:14], ("cke", k), name=("ckp", k))

        def normalise_p(u, h):
            C, top_ = width(u), 128 * (u % 8 // 4 + 1)
            if h == 0 and C < top_:
                put(PO, lambda e: e.memset(P[:, u % 2, :, 256 + C:256 + top_], 0.0), ("pt", 2 * (u - 2)),
                    ("pt", 2 * (u - 2) + 1))
            pl, pc = P[:, u % 2, h, 0:nloc(u)], P[:, u % 2, h, 256:256 + C]
            ts(PO, pl, pl, rs[:, u % 4, h, 1:2], 0.5, ALU.mult, ALU.mult, ("rs", u))
            ts(PO, pc, pc, rs[:, u % 4, h, 0:1], 0.5, ALU.mult, ALU.mult, name=("norm", 2 * u + h))

        def rope_b(u):
            for k in range(2):
                d_, s_ = slice(32 * k, 32 * k + 32), slice(32 - 32 * k, 64 - 32 * k)
                tt(PO, t2[:, :, :, d_], raw[:, u % 2, :, :, s_],
                   tB[:, u % 8, :, d_].unsqueeze(1).broadcast_to([128, 2, 2, 32]), ALU.mult, ("raw", u), ("tab", 0),
                   ("add", u - 1), name=("t2", u) if k else None)

        def split(q):
            _, gi, c, _ = chunks[q]
            w = gi % 2
            if c < 4:
                h_, l_, src = wh[:, w, c, 0:512], wl[:, w, c, 0:512], wr[:, q % 2, :]
            else:
                k0 = 2 * (c - 4)
                h_, l_ = wh[:, w, k0:k0 + 2, 512:768], wl[:, w, k0:k0 + 2, 512:768]
                src = wr[:, q % 2, :].rearrange("p (k n) -> p k n", k=2)
            ts(PO, h_, src, 1.0, 1.0, ALU.mult, ALU.mult, ("w", q), ("qk", 8 * (gi - 1) - 1),
               ("v", 8 * (gi - 1) - 1), name=("sh", q))
            tt(PO, l_, src, f32(h_), ALU.subtract, ("sh", q), name=("split", q))

        def bias_rows(gi):
            b_, r_ = bh[:, gi % 2, :], flat(br)
            ts(PO, b_, r_, 1.0, 1.0, ALU.mult, ALU.mult, ("br", gi), ("qk", 8 * (gi - 1) - 1), ("const", 0),
               name=("bhi", gi))
            ts(PO, r_, r_, cst[:, C_NR:C_NR + 1], 1.0, ALU.mult, ALU.mult, ("bhi", gi), name=("bn", gi))

        def bias_done(gi):
            b_ = bh[:, gi % 2, :]
            stt(b_, f32(b_), cst[:, C_MR:C_MR + 1], flat(br), ALU.mult, ALU.add, ("bn", gi), name=("bias", gi))

        def add_bo(t):
            a = acc[:, t % 8, :]
            tt(PO, a, a, bob[:, :], ALU.add, ("xacc", t), ("bo2", 0), name=("bo", t))

        first_loads()
        put(PO, lambda e: e.memset(onef[:, :], 1.0))
        put(PO, lambda e: e.memset(mh[:, :], -0.5), name=("ones", 0))
        put(DV, lambda e: e.tensor_copy(oner[:, :], onef[:, :]), ("ones", 0), ("const", 0))
        put(DV, lambda e: e.tensor_copy(idb[:, :], ident))
        put(DV, lambda e: e.tensor_copy(m32[:, :], cst[:, C_M32:C_M32 + 32]))
        ts(DV, isc[:, 2:4], isc[:, 0:2], 0.5, None, ALU.mult, ALU.bypass, name=("half", 0))
        put(DV, lambda e: e.reciprocal(sm[:, 14:16], isc[:, 0:2]), name=("rsc", 0))
        tt(DV, isc[:, 4:5], sm[:, 14:15], sm[:, 15:16], ALU.mult, ("rsc", 0), name=("isc", 0))

        def quant_w2():
            for kt in range(KT):
                cast8(acc[:, kt, :], 1, ("w2raw", 0), ("half", 0), *([("w2", kt - 1)] if kt else []),
                      name=("c8", kt))
                quant(w2q[:, kt, :], 1, ("c8", kt), name=("w2", kt))

        def tables():
            b8_ = [128, NT, 64]
            for j in range(2):
                w = wrow[:, j * 128:(j + 1) * 128]
                if j:
                    ts(DV, w, w, SQD, None, ALU.mult, ALU.bypass, ("table", 0), name=("wk", 0))
                tt(DV, tA[:, :, j, :], tA[:, :, j, :], w[:, 0:64].unsqueeze(1).broadcast_to(b8_), ALU.mult,
                   ("table", 0), *([("wk", 0)] if j else []))
                for k in range(2):
                    d_, s_ = slice(32 * k, 32 * k + 32), slice(32 - 32 * k, 64 - 32 * k)
                    tt(DV, tB[:, :, j, d_], tB[:, :, j, d_], w[:, s_].unsqueeze(1).broadcast_to([128, NT, 32]),
                       ALU.mult)
            w = wrow[:, 128:256]
            tt(DV, cA[:, :, :], cA[:, :, :], w[:, 0:64].unsqueeze(1).broadcast_to([128, 2, 64]), ALU.mult)
            for k in range(2):
                d_, s_ = slice(32 * k, 32 * k + 32), slice(32 - 32 * k, 64 - 32 * k)
                tt(DV, cB[:, :, d_], cB[:, :, d_], w[:, s_].unsqueeze(1).broadcast_to([128, 2, 32]), ALU.mult)
            tt(DV, wqk[:, :], wrow[:, 64:128], wrow[:, 192:256], ALU.mult)
            ts(DV, blT[:, :], blT[:, :], 0.5, None, ALU.mult, ALU.bypass, name=("bl", 0))
            qu.at["tab", 0] = qu.at["bl", 0]

        def load_wo4(n):
            src = Wo[n * 512:(n + 1) * 512, :].rearrange("(h p) n -> p h n", p=128)
            dma(lambda e: e.dma_start(acc[:, 4:8, :], src), "d_3", ("blvo", n - 1), name=("wo4", n))

        def blv_out(n):
            for h in range(4):
                mm_(bP[0][0:1, :], blT[:, 4 * n + h:4 * n + h + 1], acc[:, 4 + h, :], n + h == 0, n == 3 and h == 3,
                    ("wo4", n), ("bl", 0), name=("blvo", n) if h == 3 else None)
            if n == 3:
                put(DV, lambda e: e.tensor_copy(P[0:1, 0, 0, :], bP[0][0:1, :]), ("blvo", 3), name=("brow", 0))
                mm_(bP[1][:, :], onef[0:1, :], P[0:1, 0, 0, :], True, True, ("brow", 0), name=("ball", 0))
                tt(DV, bob[:, :], bob[:, :], bP[1][:, :], ALU.add, ("ball", 0), ("table", 0), name=("bo2", 0))

        def tile_at(s, lag):
            m = s - lag + 8
            return m // 64 * 8 + m % 64 if 0 <= m < 64 * NB and m % 64 < 8 else None

        def unit(s, lag):
            return s - lag if 0 <= s - lag < NU else None

        stages = {f.__name__: (kind, f) for kind, fs in (
            ("U", (tr, proj_qk, proj_v, scores, turn_p, values, out_proj, hi_qk, hi_p, evac_qk, squares, exp_l, exp_s,
                   hi_v, hi_c, kscale, lo_qk, pick, sums, inverse, lo_p, rope_a, rope_rest, eps_qk, rope_add, neg_r,
                   max8, mask_max, strike, neg_max, lo_v, lo_c, add_out, normalise_p, rope_b, power_qk)),
            ("T", (turn_x, entries, ffn, hi_x, cast_x, exp_w, put_et, norm_stats, normalise, lo_x, group_max, quant_x,
                   weights4, init, add_bo, power_x)),
            ("K", (ckv, turn_ck, put_kv, hi_ck, rope_ck, lo_ck, power_ck)),
            ("O", (hi_wo, lo_wo)), ("W", (split,))) for f in fs}

        def run(eng, s):
            for name, lag, *args in ORDER[eng]:
                kind, f = stages[name]
                if kind in "OW":
                    for q, c in enumerate(chunks):
                        if c[3] == s and c[0] == kind.lower():
                            f(q)
                elif kind == "U":
                    if 0 <= s - lag < NU:
                        f(s - lag, *args)
                else:
                    t = tile_at(s, lag)
                    if t is not None and (kind == "T" or t % 4 == 3):
                        f(t if kind == "T" else t // 4, *args)

        qnext = 1
        for s in range(-9, NU + 8):
            if s < -5:
                load_wo4(s + 9)
            t = tile_at(s, STORE_LAG + 1)
            if 0 <= s - STORE_LAG < NU and ((s - STORE_LAG) // 8) % 8 == 7:
                store(s - STORE_LAG)
            if t is not None:
                load_acc(t)
            while qnext < len(chunks) and chunks[qnext][3] <= s + 1:
                load_chunk(qnext)
                qnext += 1
            if s % 8 == 6 and 0 < s // 8 + 1 < NU // 8:
                load_bias(s // 8 + 1)
            t = tile_at(s + 1, 0)
            if t is not None and t >= 2:
                load_x(t)
            for eng in (PE, AC, DV, PO):
                run(eng, s)
            if s == -9:
                quant_w2()
                tables()
                bias_rows(0)
                bias_done(0)
            if s < -5:
                blv_out(s + 9)
            if s % 8 == 7 and 0 < s // 8 + 1 < NU // 8:
                bias_rows(s // 8 + 1)
                bias_done(s // 8 + 1)

        block = ctx.enter_context(nc.Block())

        @block.sync
        def _(e):
            qu.emit("sync", e)

        @block.tensor
        def _(e):
            qu.emit(PE, e)

        @block.scalar
        def _(e):
            qu.emit(AC, e)

        @block.vector
        def _(e):
            qu.emit(DV, e)

        @block.gpsimd
        def _(e):
            qu.emit(PO, e)


def constants():
    import numpy as np

    c = np.zeros((128, C_N), np.float32)
    r = np.arange(128)
    c[:, C_ID:C_ID + 128] = np.eye(128)
    cur = np.where(r[None, :] <= r[:, None], 0.0, NEG)
    prev = np.where(r[None, :] >= r[:, None], 0.0, NEG)
    c[:, C_MK:C_MK + 384] = np.concatenate([cur, prev, cur], 1)
    c[:, C_MG:C_MG + 128] = np.where(r[None, :] // 4 == r[:, None] // 4, 0.0, NEG)
    c[:, C_SEL:C_SEL + 32] = r[:, None] // 4 == np.arange(32)[None, :]
    c[0, C_MR], c[1, C_MR], c[1, C_NR] = 1.0, -1.0, 1.0
    c[:, C_M32:C_M32 + 32] = np.where(4 * np.arange(32)[None, :] + 3 <= r[:, None], 0.0, NEG)
    f = np.float32
    inv = f(1.0) / np.power(f(10000.0), np.arange(32, dtype=f) * f(2.0 / 64))

    def table(pos):
        ang = pos.astype(f)[:, None] * inv[None, :].astype(f)
        co, si = np.cos(ang).astype(f), np.sin(ang).astype(f)
        both = np.stack([np.concatenate([co, co], 1), np.concatenate([-si, si], 1)])
        return np.ascontiguousarray(both.reshape(2, -1, 128, 64).transpose(0, 2, 1, 3))

    return c, table(np.arange(SEQ)), table(np.arange(1, SEQ // 4 + 1) * 4 - 1)


_INS = ["hidden_states", "Wq", "bq", "Wcmp", "bcmp", "Wk", "bk", "Wv", "bv", "Wlk", "blk", "Wlv", "blv",
        "qn_w", "kn_w", "Wo", "bo"]


def kernel(**inputs):
    import numpy as _np
    import concourse.bacc as _bacc
    from concourse.bass_utils import run_bass_kernel_spmd as _run

    nc = _bacc.Bacc("TRN2", target_bir_lowering=False, num_devices=1, dynamic_dma_scratch_size=1024)
    given = {n: inputs["L0_attn_" + n] for n in _INS}
    for n in ("input2", "scale", "scale1"):
        given[n] = inputs["L0_ffn_" + n]
    given["consts"], given["tabs"], given["ctabs"] = constants()
    arrays, args = {}, []
    for name, v in given.items():
        a = _np.ascontiguousarray(v)
        a = a.reshape(1) if a.ndim == 0 else a
        arrays["in_" + name] = a
        args.append(nc.dram_tensor("in_" + name, a.shape, mybir.dt.from_np(a.dtype), kind="ExternalInput").ap())
    out = nc.dram_tensor("out_0", (NB, SEQ, HID), F32, kind="ExternalOutput").ap()
    build(nc, *args, out)
    r = _run(nc, [arrays], core_ids=[0])
    return r.results[0]["out_0"]
```

```python
from contextlib import ExitStack

import concourse.bass as bass
from concourse import mybir

F32 = mybir.dt.float32
F32R = mybir.dt.float32r
BF16 = mybir.dt.bfloat16
F8 = mybir.dt.float8e4
ALU = mybir.AluOpType
ACT = mybir.ActivationFunctionType

NB, SEQ, HID, NH, D = 4, 1024, 512, 16, 128
NT = SEQ // 128
KT = HID // 128
NG = NH // 2
NU = NB * NG * NT
NTT = NB * NT
NEG = -1e30
GONE = -3e38
BIG = 3.4e38
RMS_EPS = 128 * 1e-6
SQD = float(D) ** 0.5
XR, QR = 2, 6

C_ID, C_MK, C_MG, C_SEL, C_M32, C_N = 0, 128, 512, 640, 672, 704

AHEAD = 8
STORE_LAG = 4


ORDER = {
    "tensor": [
        ("proj_qk", 0, 0), ("ckv", 3), ("scores", 2, 0), ("scores", 2, 1), ("ffn", 7), ("turn_ck", 5),
        ("values", 4, 0), ("values", 4, 1), ("proj_qk", 0, 1), ("tr", 1), ("turn_p", 3, 0), ("turn_p", 3, 1),
        ("out_proj", 4, 0), ("out_proj", 4, 1), ("proj_v", 1), ("entries", 2), ("turn_x", 1),
    ],
    "scalar": [
        ("kscale", 1), ("exp_l", 2, 0), ("hi_c", 4), ("exp_s", 2, 0), ("hi_qk", 1), ("put_p", 3, 0), ("put_p", 3, 1),
        ("hi_wo", 5), ("exp_s", 2, 1), ("squares", 0), ("exp_l", 2, 1), ("hi_x", 1), ("put_et", 2), ("cast_x", 1),
        ("put_v", 1), ("exp_w", 1), ("hi_ck", 4), ("put_kv", 2),
    ],
    "vector": [
        ("group_max", 2), ("eps_qk", 1), ("rope_a", 1), ("sums", 3), ("norm_stats", 1), ("rope_add", 1),
        ("inverse", 3), ("lo_x", 2), ("weights4", 2), ("mask_cmp", 2, 0), ("mask_max", 2, 0), ("max8", 2, 0),
        ("mask_max", 2, 1), ("neg_max", 2, 0), ("strike", 2, 0), ("normalise", 1), ("lo_ck", 5), ("mask_cmp", 2, 1),
        ("init", 7), ("lo_c", 4), ("max8", 2, 1), ("put_qk", 0), ("neg_max", 2, 1), ("pick", 2, 0), ("strike", 2, 1),
        ("lo_qk", 1), ("add_out", 4), ("rope_ck", 4), ("quant_x", 2), ("lo_wo", 19), ("neg_r", 1), ("pick", 2, 1),
        ("rope_rest", 0),
    ],
    "gpsimd": [
        ("add_bo", 6), ("rope_b", 0), ("power_ck", 4), ("split", 0), ("power_x", 0), ("power_qk", 0),
        ("normalise_p", 2, 0), ("normalise_p", 2, 1),
    ],
}


class Queues:

    def __init__(self, sem):
        self.sem, self.ops, self.n, self.at = sem, {}, {}, {}

    def put(self, eng, fn, *waits, name=None, quiet=False):
        self.ops.setdefault(eng, []).append((fn, waits, None if quiet else eng, 1))
        if not quiet:
            self.n[eng] = self.n.get(eng, 0) + 1
        if name is not None:
            assert not quiet and name not in self.at, name
            self.at[name] = (eng, self.n[eng])

    def dma(self, fn, stream, *waits, name=None):
        self.ops.setdefault("sync", []).append((fn, waits, stream, 16))
        self.n[stream] = self.n.get(stream, 0) + 16
        if name is not None:
            self.at[name] = (stream, self.n[stream])

    def emit(self, eng, e):
        seen = {}
        for fn, waits, on, v in self.ops.get(eng, []):
            need = {}
            for w in waits:
                if not isinstance(w[1], int) or w[1] >= 0:
                    s, c = self.at[w]
                    need[s] = max(need.get(s, 0), c)
            for s, c in need.items():
                if seen.get(s, 0) < c:
                    e.wait_ge(self.sem(s), c)
                    seen[s] = c
            i = fn(e)
            if on is not None:
                i.then_inc(self.sem(on), v)
        for s in sorted(k for k in self.n if k.startswith("d_")) if eng == "sync" else []:
            e.wait_ge(self.sem(s), self.n[s])


def build(nc, x, Wq, bq, Wcmp, bcmp, Wk, bk, Wv, bv, Wlk, blk, Wlv, blv, qnw, knw, Wo, bo,
          W2, sc0, sc1, consts, tabs, ctabs, out):
    ctx = ExitStack()
    S = {}

    def sb(name, shape, dt=F32):
        return ctx.enter_context(nc.sbuf_tensor(name, shape, dt))

    def ps(name, shape):
        return ctx.enter_context(nc.psum_tensor(name, shape, F32))

    def sem(name):
        if name not in S:
            S[name] = ctx.enter_context(nc.semaphore("s_" + name))
        return S[name]

    with ctx:
        xh = sb("xh", [128, KT, SEQ], F32R)
        xl = sb("xl", [128, KT, SEQ], F32R)
        wr = sb("wr", [128, 2, 512])
        wh = sb("wh", [128, 2, KT, 768], F32R)
        wl = sb("wl", [128, 2, KT, 768], F32R)
        woh = sb("woh", [128, 2, 512], F32R)
        wol = sb("wol", [128, 2, 512], F32R)
        acc = sb("acc", [128, NT, 512])
        qkh = sb("qkh", [128, 3, 2, 2, 128], F32R)
        qf = sb("qf", [128, 2, 2, 128])
        ckf = sb("ckf", [128, 2, 128])
        qkl = sb("qkl", [128, 3, 2, 2, 128], F32R)
        v_ = sb("v", [128, 4, 2, 128])
        raw = sb("raw", [128, 2, 2, 2, 128])
        t1 = sb("t1", [128, 2, 2, 64])
        t2 = sb("t2", [128, 2, 2, 64])
        tA = sb("tA", [128, NT, 2, 64])
        tB = sb("tB", [128, NT, 2, 64])
        cA = sb("cA", [128, 2, 64])
        cB = sb("cB", [128, 2, 64])
        wqk = sb("wqk", [128, 64])
        P = sb("P", [128, 2, 2, 512])
        es = sb("es", [128, 2, 256])
        rp = sb("rp", [128, 2, 256])
        pt = sb("pt", [128, 2, 512])
        ch = sb("ch", [128, 2, 2, 128], F32R)
        cl = sb("cl", [128, 2, 2, 128], F32R)
        ckh = sb("ckh", [128, 2, 256], F32R)
        ckl = sb("ckl", [128, 2, 256], F32R)
        cv = sb("cv", [128, 2, 2, 128])
        xt = sb("xt", [128, XR, 512])
        q8 = sb("q8", [128, QR, 512], BF16)
        a8 = sb("a8", [128, 512], F8)
        b8 = sb("b8", [128, 512], F8)
        qa = sb("qa", [128, 512], BF16)
        qb = sb("qb", [128, 512], BF16)
        qaw = sb("qaw", [128, 512], BF16)
        qbw = sb("qbw", [128, 512], BF16)
        w2q = sb("w2q", [128, KT, 512], BF16)
        et = sb("et", [128, KT, 128])
        wkv = sb("wkv", [128, KT, 256])
        bkv = sb("bkv", [1, 256])
        ckr = sb("ckr", [128, 128])
        ct = sb("ct", [128, 2, 64])
        wcb = sb("wcb", [128, 512])
        bob = sb("bob", [128, 512])
        br = sb("br", [128, 2, 2, 2, 128])
        cst = sb("cst", [128, C_N])
        a8w = sb("a8w", [128, KT, 512], F8)
        b8w = sb("b8w", [128, KT, 512], F8)
        onef = sb("onef", [128, 128])
        junk = sb("junk", [128, 5, 128], BF16)
        junkd = sb("junkd", [128, 512], BF16)
        dg = sb("dg", [128, 128])
        eg = sb("eg", [128, 128])
        wm = sb("wm", [128, 32])
        sm = sb("sm", [128, 16])
        st = sb("st", [128, 12])
        mh = sb("mh", [128, 4])
        ss = sb("ss", [128, 4, 4])
        r4 = sb("r4", [128, 4, 4])
        ngr = sb("ngr", [128, 4, 2])
        mm = sb("mm", [128, 4, 2, 9])
        nm = sb("nm", [128, 4, 2, 2])
        su = sb("su", [128, 4, 2, 2])
        rs = sb("rs", [128, 4, 2, 2])
        blT = sb("blT", [128, NH])
        isc = sb("isc", [128, 5])
        bcm = sb("bcm", [128, 1])
        wrow = P[:, 1, 0, 0:256]

        bQK = ps("bQK", [128, 512])
        bVC = ps("bVC", [128, 512])
        bT = ps("bT", [128, 512])
        bS = [ps("bS0", [128, 512]), ps("bS1", [128, 512])]
        bP = [ps("bP0", [128, 512]), ps("bP1", [128, 512])]
        bY = ps("bY", [128, 512])

        ident = cst[:, C_ID:C_ID + 128]

        def flat(ap):
            return ap.rearrange("p a b c -> p (a b c)")

        def f32(ap):
            return ap.bitcast(F32)

        qu = Queues(sem)
        put, dma = qu.put, qu.dma
        PE, AC, DV, PO = "tensor", "scalar", "vector", "gpsimd"

        def slots_of(u):
            s = u % 3
            return [s] if u % 8 == 0 else [0, 2] if s == 0 else [s - 1, s]

        def units_of(u):
            return [u] if u % 8 == 0 else [u, u - 1] if u % 3 == 0 else [u - 1, u]

        def mask_of(u):
            a = C_MK + (0 if u % 3 == 0 or u % 8 == 0 else 128)
            return cst[:, a:a + nloc(u)]

        def width(u):
            return 32 * (u % 8 + 1)

        def nloc(u):
            return 128 if u % 8 == 0 else 256

        def pblocks(u):
            return ([0] if u % 8 == 0 else [0, 1]) + ([2] if u % 8 < 4 else [2, 3])

        chunks = []
        for s in range(-8, NU):
            gi, i = s // 8, s % 8
            if i == 3 and gi >= 0:
                chunks += [("o", gi, 0, s), ("o", gi, 1, s)]
            if i != 3 and i != 7 and gi + 1 < NU // 8:
                chunks.append(("w", gi + 1, i if i < 3 else i - 1, s))
        where = {(k, gi, c): q for q, (k, gi, c, _) in enumerate(chunks)}

        def load_x(t):
            dma(lambda e: e.dma_start(xt[:, t % XR, :], x[t // 8, (t % 8) * 128:(t % 8 + 1) * 128, :]),
                f"d_x{t % XR}", ("et", t - XR), name=("x", t))

        def load_chunk(q):
            k, gi, c, _ = chunks[q]
            g = gi % NG
            free = [("wohi", q - 2), ("wolo", q - 2)] if q >= 2 and chunks[q - 2][0] == "o" else [("split", q - 2)]
            dst, stream = wr[:, q % 2, :], f"d_w{q % 2}"
            if k == "o":
                h = 2 * g + c
                dma(lambda e: e.dma_start(dst, Wo[h * 128:(h + 1) * 128, :]), stream, *free, name=("w", q))
            elif c < 4:
                d4 = dst.rearrange("p (h k d) -> p h k d", h=2, k=2)
                for j, w in enumerate((Wq, Wlk)):
                    src = w[c * 128:(c + 1) * 128, g * 256:(g + 1) * 256].rearrange("p (h d) -> p h d", h=2)
                    dma(lambda e, j=j, src=src: e.dma_start(d4[:, :, j, :], src), stream, *free,
                        name=("w", q) if j else None)
            else:
                k0 = 2 * (c - 4)
                src = Wlv[k0 * 128:(k0 + 2) * 128, g * 256:(g + 1) * 256].rearrange("(k p) n -> p k n", p=128)
                dma(lambda e: e.dma_start(dst.rearrange("p (k n) -> p k n", k=2), src), stream, *free,
                    name=("w", q))

        def load_bias(gi):
            g = gi % NG
            for j, w in enumerate((bq, blk)):
                for h in range(2):
                    o = g * 256 + h * 128
                    src = w[o:o + 128].rearrange("(a d) -> a d", a=1).broadcast_to([128, 128])
                    dma(lambda e, h=h, j=j, src=src: e.dma_start(br[:, gi % 2, h, j, :], src), f"d_b{gi % 2}", ("raw", 8 * (gi - 1) - 1),
                        name=("br", gi) if h + j == 2 else None)

        def bc(ap, n):
            return ap.rearrange("(a n) -> a n", a=1).broadcast_to([128, n])

        def wo4(n):
            if n == 0:
                return [acc[:, 4 + h, :] for h in range(4)]
            if n == 3:
                return [flat(cv[:, :, :, :]), flat(qf[:, :, :, :]), es[:, :, :].rearrange("p a b -> p (a b)"),
                        rp[:, :, :].rearrange("p a b -> p (a b)")]
            if n == 1:
                return [v_[:, 2 * h:2 * h + 2].rearrange("p a b c -> p (a b c)") for h in range(2)] + [
                    flat(raw[:, h]) for h in range(2)]
            return [pt[:, h, :] for h in range(2)] + [P[:, 0, h, :] for h in range(2)]

        def load_wo4(n):
            for h, dst in enumerate(wo4(n)):
                src = Wo[(4 * n + h) * 128:(4 * n + h + 1) * 128, :]
                dma(lambda e, dst=dst, src=src: e.dma_start(dst, src), f"d_l{n}", name=("wo4", n) if h == 3 else None)

        def first_loads():
            def load(stream, dst, src, name=None, **kw):
                dma(lambda e: e.dma_start(dst, src, **kw), stream, name=name)

            load("d_c", cst[:, :], consts)
            load("d_c", wcb[:, :], Wcmp.rearrange("n a -> a n").broadcast_to([128, 512]))
            load("d_c", bcm[:, :], bc(bcmp, 1))
            load("d_c", isc[:, 0:1], bc(sc0, 1))
            load("d_c", isc[:, 1:2], bc(sc1, 1), name=("const", 0))
            load_x(0)
            load("d_2", acc[:, 0:KT, :], W2.rearrange("(k p) n -> p k n", p=128), name=("w2raw", 0))
            load("d_3", blT[:, :], blv.rearrange("(h d) -> d h", d=128), name=("blT", 0),
                 allow_slow_non_contiguous=True)
            load_chunk(0)
            load_wo4(0)
            load_wo4(1)
            load_x(1)
            load("d_t", wrow[:, 0:128], bc(qnw, 128))
            load("d_t", wrow[:, 128:256], bc(knw, 128))
            for j in range(2):
                load("d_t", tA[:, :, j, :], tabs[0])
                load("d_t", tB[:, :, j, :], tabs[1])
            load("d_t", cA[:, :, :], ctabs[0])
            load("d_t", cB[:, :, :], ctabs[1])
            load("d_t", wkv[:, :, 0:128], Wk.rearrange("(k p) n -> p k n", p=128))
            load("d_t", wkv[:, :, 128:256], Wv.rearrange("(k p) n -> p k n", p=128))
            load("d_t", bkv[:, 0:128], bk.rearrange("(a n) -> a n", a=1))
            load("d_t", bkv[:, 128:256], bv.rearrange("(a n) -> a n", a=1))
            load("d_t", bob[:, :], bc(bo, 512), name=("table", 0))
            load_wo4(2)
            load_wo4(3)
            load_bias(0)

        def load_acc(t):
            wait = [("store", t - 8)] if t >= 8 else [("c8", KT - 1), ("blvo", 3)]
            dma(lambda e: e.dma_start(acc[:, t % 8, :], x[t // 8, (t % 8) * 128:(t % 8 + 1) * 128, :]),
                f"d_a{t % 8}", *wait, name=("xacc", t))

        def store(u):
            b, i = u // 64, u % 8
            dma(lambda e: e.dma_start(out[b, i * 128:(i + 1) * 128, :], acc[:, i, :]), f"d_o{i}", ("acc", u),
                name=("store", b * 8 + i))

        free = {"T": [], "Y": [], "V": []}

        def mm_(dst, a, b, start, stop, *waits, name=None):
            put(PE, lambda e: e.matmul(dst, a, b, start=start, stop=stop), *waits, name=name, quiet=name is None)

        def turn_(dst, src, *waits, name=None):
            put(PE, lambda e: e.transpose(dst, src, ident), *waits, name=name, quiet=name is None)

        def three(dst, ah, al, bh_, bl_, first, last, *waits, name=None):
            mm_(dst, ah, bh_, first, False, *waits)
            mm_(dst, ah, bl_, False, False)
            mm_(dst, al, bh_, False, last, name=name)

        def tr(u):
            for k in range(4):
                turn_(bT[:, k * 128:(k + 1) * 128], raw[:, u % 2, k // 2, k % 2, :], ("kscale", u), ("add", u), ("const", 0),
                      *free["T"], name=("tr", u) if k == 3 else None)
            free["T"] = [("hi_qk", u), ("lo_qk", u)]

        def proj_qk(u, half):
            gi, i, w = u // 8, u % 8, u // 8 % 2
            waits = [("raw", u - 1), ("split", where["w", gi, 3])]
            if gi % NG == 0:
                waits += [("hi_x", u // 64 * 8 + i), ("lo_x", u // 64 * 8 + i)]
            c = slice(i * 128, (i + 1) * 128)
            for kt in (0, 1) if half == 0 else (2, 3):
                three(bQK[:, :], xh[:, kt, c], xl[:, kt, c], wh[:, w, kt, 0:512], wl[:, w, kt, 0:512],
                      kt == 0, kt == 3, *waits, name=("qk", u) if kt == 3 else None)

        def proj_v(u):
            gi, i, w = u // 8, u % 8, u // 8 % 2
            waits = [*free["V"], ("split", where["w", gi, 5])]
            if gi % NG == 0:
                waits += [("hi_x", u // 64 * 8 + i), ("lo_x", u // 64 * 8 + i)]
            free["V"] = [("put_v", u)]
            c = slice(i * 128, (i + 1) * 128)
            for kt in range(KT):
                three(bVC[:, 0:256], xh[:, kt, c], xl[:, kt, c], wh[:, w, kt, 512:768], wl[:, w, kt, 512:768],
                      kt == 0, kt == KT - 1, *waits, name=("v", u) if kt == KT - 1 else None)

        def scores(u, h):
            b, i, C = u // 64, u % 8, width(u)
            k = 2 * b + i // 4
            waits = [("hi_qk", u), ("lo_qk", u), ("hi_ck", k), ("lo_ck", k), ("mr", 2 * (u - 1) + h),
                     ("es", 2 * (u - 1) + h)]
            sl = slots_of(u)
            keys = slice(sl[0], sl[-1] + 1, max(sl[-1] - sl[0], 1))
            q_, ql_ = qkh[:, u % 3, h, 0, :], qkl[:, u % 3, h, 0, :]
            three(bS[h][:, 0:nloc(u)], q_, ql_, qkh[:, keys, h, 1, :], qkl[:, keys, h, 1, :], True, True, *waits)
            cmp = bS[h][:, 256:256 + C]
            if i < 4:
                mm_(cmp, qf[:, u % 2, h, :], ckf[:, b % 2, 0:C], True, True, name=("s", 2 * u + h))
                return
            mm_(cmp, q_, ckh[:, b % 2, 0:C], True, False)
            mm_(cmp, q_, ckl[:, b % 2, 0:C], False, False)
            mm_(cmp, ql_, ckh[:, b % 2, 0:C], False, True, name=("s", 2 * u + h))

        def turn_p(u, h):
            a = 2 * u + h
            bl = pblocks(u)
            for n, k in enumerate(bl):
                turn_(bP[h][:, n * 128:(n + 1) * 128], P[:, u % 2, h, k * 128:(k + 1) * 128], ("norm", a),
                      ("p", a - 2), name=("pt", a) if n == len(bl) - 1 else None)

        def values(u, h):
            a, b, i = 2 * u + h, u // 64, u % 8
            waits = [("p", a)]
            if h == 0:
                waits += [("p", a + 1), ("put_v", u), ("cv", 2 * b + i // 4), *free["V"]]
                free["V"] = [("hi_c", u), ("lo_c", u)]
            ts_ = units_of(u)
            if h == 0:
                for n in range(i // 4 + 1):
                    c = slice((len(ts_) + n) * 128, (len(ts_) + n + 1) * 128)
                    mm_(bVC[:, 256:512], cv[:, b % 2, n, :], pt[:, :, c], n == 0, False, *waits)
            for n, t in enumerate(ts_):
                last = n == len(ts_) - 1
                mm_(bVC[:, 256 + h * 128:384 + h * 128], v_[:, t % 4, h, :], pt[:, h, n * 128:(n + 1) * 128],
                    False, last and h == 1, *waits, name=("c", a) if last else None)

        def out_proj(u, h):
            gi = u // 8
            waits = [("hi_c", u), ("lo_c", u), ("wolo", where["o", gi, 1]), ("wohi", where["o", gi, 1])]
            three(bY[:, :], ch[:, u % 2, h, :], cl[:, u % 2, h, :], woh[:, h, :], wol[:, h, :], h == 0, h == 1,
                  *waits, *(free["Y"] if h == 0 else ()), name=("wo", u) if h else None)
            free["Y"] = [("acc", u)]

        def turn_x(t):
            for kt in range(KT):
                turn_(bT[:, kt * 128:(kt + 1) * 128], xt[:, t % XR, kt * 128:(kt + 1) * 128], ("xn", t),
                      *free["T"], name=("xt", t) if kt == KT - 1 else None)
            free["T"] = [("hi_x", t), ("b8", t), ("lo_x", t)]
            mm_(bY[:, 0:128], onef[:, :], dg[:, :], True, True, ("dg", t), *free["Y"], name=("bc", t))
            free["Y"] = [("eg", t)]

        def entries(t):
            for kt in range(KT):
                mm_(bY[:, kt * 32:(kt + 1) * 32], xt[:, t % XR, kt * 128:(kt + 1) * 128], wm[:, :], True, True,
                    ("wm", t), *free["Y"], name=("et", t) if kt == KT - 1 else None)
            free["Y"] = [("put_et", t)]

        def ckv(k):
            for kt in range(KT):
                mm_(bY[:, 0:256], et[:, kt, :], wkv[:, kt, :], kt == 0, False, ("put_et", 4 * k + 3), *free["Y"])
            mm_(bY[:, 0:256], onef[0:1, :], bkv[:, :], False, True, name=("kv", k))
            free["Y"] = [("css", k)]

        def turn_ck(k):
            turn_(bT[:, 0:128], ckr[:, 0:128], ("cks", k), *free["T"], name=("ct", k))
            free["T"] = [("hi_ck", k), ("lo_ck", k)]

        def ffn(t):
            for kt in range(KT):
                mm_(bY[:, :], q8[:, t % QR, kt * 128:(kt + 1) * 128], w2q[:, kt, :], kt == 0, kt == KT - 1,
                    ("q8", t), *free["Y"], name=("ff", t) if kt == KT - 1 else None)
            free["Y"] = [("init", t)]

        def act(dst, src, func, *waits, name=None, **kw):
            put(AC, lambda e: e.activation(dst, src, func, **kw), *waits, name=name)

        def hi_qk(u):
            free_ = [("s", 2 * (u - 2)), ("s", 2 * (u - 2) + 1)]
            if u % 8 < 4:
                src = bT[:, :].rearrange("p (h k c) -> p h k c", h=2, k=2)[:, :, 0, :]
                act(qf[:, u % 2], src, ACT.Copy, ("tr", u), *free_)
            act(flat(qkh[:, u % 3]), bT[:, :], ACT.Copy, ("tr", u), *free_, ("lo_qk", u - 3), name=("hi_qk", u))

        def put_p(u, h):
            n = len(pblocks(u)) * 128
            act(pt[:, h, 0:n], bP[h][:, 0:n], ACT.Copy, ("pt", 2 * u + h), ("c", 2 * (u - 1)),
                ("c", 2 * (u - 1) + h), name=("p", 2 * u + h))

        def squares(u):
            for k in range(4):
                act(junk[:, k, :], raw[:, u % 2, k // 2, k % 2, :], ACT.Square, ("raw", u), ("sq", u - 1),
                    accum_out=ss[:, u % 4, k:k + 1], name=("sq", u) if k == 3 else None)

        def kscale(u):
            for h in range(2):
                k_ = raw[:, u % 2, h, 1, :]
                act(k_, k_, ACT.Copy, ("r4", u), ("add", u), ("krest", u), scale=r4[:, u % 4, 2 * h + 1:2 * h + 2],
                    name=("kscale", u) if h else None)

        def exp_l(u, h):
            pl = P[:, u % 2, h, 0:nloc(u)]
            act(pl, pl, ACT.Exp, ("nm", 2 * u + h), scale=r4[:, u % 4, 2 * h:2 * h + 1], bias=nm[:, u % 4, h, 1:2],
                accum_out=su[:, u % 4, h, 1:2], name=("el", 2 * u + h))

        def exp_s(u, h):
            C = width(u)
            act(es[:, h, 0:C], bS[h][:, 256:256 + C], ACT.Exp, ("nm", 2 * u + h), ("mr", 2 * u + h),
                ("stt", 2 * (u - 1) + h),
                scale=r4[:, u % 4, 2 * h:2 * h + 1], bias=nm[:, u % 4, h, 0:1], name=("es", 2 * u + h))

        def put_v(u):
            act(v_[:, u % 4].rearrange("p a b -> p (a b)"), bVC[:, 0:256], ACT.Copy, ("v", u),
                ("c", 2 * (u - 3)), ("c", 2 * (u - 3) + 1), name=("put_v", u))

        def hi_c(u):
            act(ch[:, u % 2].rearrange("p a b -> p (a b)"), bVC[:, 256:512], ACT.Copy, ("c", 2 * u), ("c", 2 * u + 1),
                ("wo", u - 2), name=("hi_c", u))

        def hi_wo(q):
            gi, c = chunks[q][1:3]
            act(woh[:, c, :], wr[:, q % 2, :], ACT.Copy, ("w", q), ("wo", 8 * gi - 1), name=("wohi", q))

        def hi_x(t):
            b, j = t // 8, t % 8
            src = bT[:, :].rearrange("p (k c) -> p k c", k=KT)
            act(xh[:, :, j * 128:(j + 1) * 128], src, ACT.Copy, ("xt", t),
                ("qk", (b - 1) * 64 + 56 + j), ("v", (b - 1) * 64 + 56 + j),
                name=("hi_x", t))

        def cast8(a_, b_, src, i, *waits, name):
            act(a_, src, ACT.Copy, *waits, scale=isc[:, i:i + 1], saturate=False)
            act(b_, src, ACT.Copy, scale=isc[:, i + 2:i + 3], saturate=False, name=name)

        def cast_x(t):
            cast8(a8[:, :], b8[:, :], bT[:, :], 0, ("xt", t), ("q8", t - 1), ("half", 0), name=("b8", t))

        def exp_w(t):
            act(eg[:, :], eg[:, :], ACT.Exp, ("neg", t), ("wtok", t - 1), bias=sm[:, 3:4], accum_out=sm[:, 4:5])
            act(sm[:, 5:6], sm[:, 2:3], ACT.Exp, bias=sm[:, 3:4], name=("ew", t))

        def put_et(t):
            act(et[:, :, (t % 4) * 32:(t % 4 + 1) * 32], bY[:, 0:128].rearrange("p (k c) -> p k c", k=KT),
                ACT.Copy, ("et", t), ("kv", t // 4 - 1), name=("put_et", t))

        def put_kv(k):
            b = k // 2
            act(ckr[:, :], bY[:, 0:128], ACT.Copy, ("kv", k), ("ct", k - 1), name=("kvr", k))
            act(cv[:, b % 2, k % 2, :], bY[:, 128:256], ACT.Copy, ("c", 2 * (64 * (b - 1) - 1)), name=("cv", k))
            act(junk[:, 4, :], bY[:, 0:128], ACT.Square, ("css", k - 1), accum_out=sm[:, 12:13], name=("css", k))

        def hi_ck(k):
            b = k // 2
            if k % 2 == 0:
                act(ckf[:, b % 2, :], bT[:, 0:128], ACT.Copy, ("ct", k), ("s", 2 * (64 * (b - 1) - 1)),
                    ("s", 2 * (64 * (b - 1) - 1) + 1))
            act(ckh[:, b % 2, (k % 2) * 128:(k % 2 + 1) * 128], bT[:, 0:128], ACT.Copy, ("ct", k),
                ("s", 2 * (64 * (b - 1) - 1) + 1), name=("hi_ck", k))

        def tt(eng, dst, a, b, op, *waits, name=None):
            put(eng, lambda e: e.tensor_tensor(dst, a, b, op), *waits, name=name)

        def ts(eng, dst, a, s1, s2, op0, op1, *waits, name=None, **kw):
            put(eng, lambda e: e.tensor_scalar(dst, a, s1, s2, op0, op1, **kw), *waits, name=name)

        def stt(dst, a, s, b, op0, op1, *waits, name=None, **kw):
            put(DV, lambda e: e.scalar_tensor_tensor(out=dst, in0=a, scalar=s, in1=b, op0=op0, op1=op1, **kw),
                *waits, name=name)

        def lo(dst, src, hi, *waits, name):
            tt(DV, dst, src, f32(hi), ALU.subtract, *waits, name=name)

        def lo_qk(u):
            lo(flat(qkl[:, u % 3]), bT[:, :], flat(qkh[:, u % 3]), ("hi_qk", u), ("lo_qk", u - 1), name=("lo_qk", u))

        def pick(u, h):
            C = width(u)
            stt(P[:, u % 2, h, 256:256 + C], rp[:, h, 0:C], GONE, es[:, h, 0:C], ALU.is_equal, ALU.mult,
                ("es", 2 * u + h), ("mr", 2 * u + h), ("pt", 2 * (u - 2) + h), accum_out=su[:, u % 4, h, 0:1],
                name=("stt", 2 * u + h))

        def sums(u):
            if u % 8:
                return
            ts(DV, rs[:, u % 4], su[:, u % 4], 1e-9, None, ALU.max, ALU.bypass, ("stt", 2 * u), ("stt", 2 * u + 1),
               ("el", 2 * u), ("el", 2 * u + 1), name=("rs0", u))

        def inverse(u):
            put(DV, lambda e: e.reciprocal(rs[:, u % 4], (su if u % 8 else rs)[:, u % 4]), ("stt", 2 * u),
                ("stt", 2 * u + 1), ("el", 2 * u), ("el", 2 * u + 1), *([] if u % 8 else [("rs0", u)]), name=("rs", u))

        def put_qk(u):
            b_ = br[:, u // 8 % 2].rearrange("p a b c -> p (a b c)")
            tt(DV, flat(raw[:, u % 2]), bQK[:, :], b_, ALU.add, ("qk", u), ("br", u // 8), ("tr", u - 2),
               name=("raw", u))

        def rope_a(u):
            b_ = [128, 2, 2, 64]
            tt(DV, t1[:, :, :, :], raw[:, u % 2, :, :, 0:64], tA[:, u % 8].unsqueeze(1).broadcast_to(b_), ALU.mult,
               ("raw", u), ("tab", 0), ("add", u - 1), name=("t1", u))

        def rope_rest(u):
            kr = raw[:, u % 2, :, 1, 64:128]
            tt(DV, kr, kr, wqk[:, :].unsqueeze(1).broadcast_to([128, 2, 64]), ALU.mult, ("sq", u), ("tab", 0),
               name=("krest", u))

        def eps_qk(u):
            ts(DV, ss[:, u % 4], ss[:, u % 4], RMS_EPS, None, ALU.add, ALU.bypass, ("sq", u), name=("veps", u))

        def rope_add(u):
            tt(DV, raw[:, u % 2, :, :, 0:64], t1[:, :, :, :], t2[:, :, :, :], ALU.add, ("sq", u), ("t1", u),
               ("t2", u), name=("add", u))

        def neg_r(u):
            if u % 8:
                return
            ts(DV, ngr[:, u % 4], r4[:, u % 4, 0:4:2], -1.0, None, ALU.mult, ALU.bypass, ("r4", u), name=("ngr", u))

        def mask_cmp(u, h):
            d_ = bS[h][:, 256 + width(u) - 32:256 + width(u)]
            tt(DV, d_, d_, cst[:, C_M32:C_M32 + 32], ALU.add, ("s", 2 * u + h), name=("mc", 2 * u + h))

        def max8(u, h):
            put(DV, lambda e: e.max(mm[:, u % 4, h, 0:8], bS[h][:, 256:256 + width(u)]), ("mc", 2 * u + h),
                name=("m8", 2 * u + h))

        def mask_max(u, h):
            put(DV, lambda e: e.tensor_tensor_reduce(P[:, u % 2, h, 0:nloc(u)], bS[h][:, 0:nloc(u)], mask_of(u), 1.0,
                                                     GONE, ALU.add, ALU.max, mm[:, u % 4, h, 8:9]),
                ("s", 2 * u + h), ("pt", 2 * (u - 2) + h), name=("ttr", 2 * u + h))

        def strike(u, h):
            C, a = width(u), 2 * u + h
            put(DV, lambda e: e.match_replace(rp[:, h, 0:C], mm[:, u % 4, h, 0:8], bS[h][:, 256:256 + C], GONE),
                ("m8", a), ("ttr", a), ("stt", a - 2), name=("mr", a))

        def neg_max(u, h):
            m = mm[:, u % 4, h, 0:9:8]
            if u % 8 == 0:
                r_, s_, op, after = ngr[:, u % 4, h:h + 1], NEG / 10, ALU.max, ("ngr", u)
            else:
                r_, s_, op, after = r4[:, u % 4, 2 * h:2 * h + 1], -1.0, ALU.mult, ("r4", u)
            ts(DV, nm[:, u % 4, h], m, s_, r_, op, ALU.mult, ("m8", 2 * u + h), ("ttr", 2 * u + h), after,
               name=("nm", 2 * u + h))

        def lo_c(u):
            fl_ = lambda a: a[:, u % 2].rearrange("p a b -> p (a b)")
            lo(fl_(cl), bVC[:, 256:512], fl_(ch), ("hi_c", u), ("lo_c", u - 1), name=("lo_c", u))

        def add_out(u):
            a = acc[:, u % 8, :]
            first = [("init", u // 64 * 8 + u % 8)] if (u // 8) % 8 == 0 else [("acc", u - 8)]
            tt(DV, a, bY[:, :], a, ALU.add, ("wo", u), *first, name=("acc", u))

        def lo_wo(q):
            c = chunks[q][2]
            lo(wol[:, c, :], wr[:, q % 2, :], woh[:, c, :], ("wohi", q), name=("wolo", q))

        def norm_stats(t):
            xs = xt[:, t % XR, :]
            put(DV, lambda e: e.bn_stats(st[:, 0:6], xs), ("x", t), ("xn", t - 1), name=("bs", t))
            put(DV, lambda e: e.bn_aggr(st[:, 6:8], st[:, 0:6]), ("bs", t), name=("ba", t))
            ts(DV, st[:, 8:9], st[:, 7:8], 1e-5, None, ALU.add, ALU.bypass, ("ba", t), ("rstd", t - 1), name=("xv", t))

        def normalise(t):
            xs = xt[:, t % XR, :]
            ts(DV, xs, xs, st[:, 6:7], st[:, 9:10], ALU.subtract, ALU.mult, ("rstd", t), ("ba", t), name=("xn", t))
            put(DV, lambda e: e.tensor_tensor_reduce(junkd[:, :], xs, wcb[:, :], 1.0, 0.0, ALU.mult, ALU.add,
                                                     sm[:, 0:1]), ("xn", t), ("wl", t - 1), name=("wl", t))
            ts(DV, sm[:, 2:3], sm[:, 0:1], bcm[:, 0:1], None, ALU.add, ALU.bypass, ("wl", t), ("ew", t - 1),
               name=("wlb", t))
            ts(DV, dg[:, :], ident, sm[:, 2:3], None, ALU.mult, ALU.bypass, ("wlb", t), ("bc", t - 1),
               name=("dg", t))

        def lo_x(t):
            j = t % 8
            c = slice(j * 128, (j + 1) * 128)
            lo(xl[:, :, c], bT[:, :].rearrange("p (k c) -> p k c", k=KT), xh[:, :, c], ("hi_x", t),
               ("b8", t), name=("lo_x", t))

        def group_max(t):
            put(DV, lambda e: e.tensor_tensor_reduce(eg[:, :], bY[:, 0:128], cst[:, C_MG:C_MG + 128], 1.0, GONE,
                                                     ALU.add, ALU.max, sm[:, 9:10]),
                ("bc", t), ("ew", t - 1), name=("eg", t))
            ts(DV, sm[:, 3:4], sm[:, 9:10], -1.0, None, ALU.mult, ALU.bypass, ("eg", t), name=("neg", t))

        def quant(dst, a_, b_, qa, qb, *waits, name):
            ts(DV, qa[:, :], a_, 240.0, -240.0, ALU.min, ALU.max, *waits)
            ts(DV, qb[:, :], b_, 120.0, -120.0, ALU.min, ALU.max, name=("qb", name))
            tt(DV, qb[:, :], b_, qb[:, :], ALU.subtract, ("qb", name), name=("qd", name))
            stt(dst, qb[:, :], 2.0, qa[:, :], ALU.mult, ALU.add, ("qd", name), name=("qs", name))
            ts(DV, qb[:, :], dst, BIG / 450.0, 0.0, ALU.mult, ALU.mult, ("qs", name), name=("qn", name))
            tt(DV, dst, dst, qb[:, :], ALU.add, ("qn", name), name=name)

        def quant_x(t):
            quant(q8[:, t % QR, :], a8[:, :], b8[:, :], qa, qb, ("b8", t), ("ff", t - QR), name=("q8", t))

        def weights4(t):
            put(DV, lambda e: e.reciprocal(sm[:, 10:11], sm[:, 4:5]), ("ew", t), name=("re", t))
            tt(DV, sm[:, 11:12], sm[:, 10:11], sm[:, 5:6], ALU.mult, ("re", t), name=("wtok", t))
            ts(DV, wm[:, :], cst[:, C_SEL:C_SEL + 32], sm[:, 11:12], None, ALU.mult, ALU.bypass, ("wtok", t),
               ("et", t - 1), name=("wm", t))

        def init(t):
            a = acc[:, t % 8, :]
            stt(a, bY[:, :], isc[:, 4:5], a, ALU.mult, ALU.add, ("ff", t), ("bo", t), ("isc", 0), name=("init", t))

        def rope_ck(k):
            ts(DV, sm[:, 13:14], sm[:, 12:13], RMS_EPS, None, ALU.add, ALU.bypass, ("css", k), name=("cke", k))
            tt(DV, ct[:, 0, :], ckr[:, 0:64], cA[:, k % 2, :], ALU.mult, ("kvr", k), ("tab", 0), ("cadd", k - 1))
            tt(DV, ct[:, 1, 0:32], ckr[:, 32:64], cB[:, k % 2, 0:32], ALU.mult)
            tt(DV, ct[:, 1, 32:64], ckr[:, 0:32], cB[:, k % 2, 32:64], ALU.mult, name=("cm", k))
            tt(DV, ckr[:, 64:128], ckr[:, 64:128], wqk[:, :], ALU.mult, name=("crest", k))
            tt(DV, ckr[:, 0:64], ct[:, 0, :], ct[:, 1, :], ALU.add, ("cm", k), name=("cadd", k))
            ts(DV, ckr[:, 0:128], ckr[:, 0:128], sm[:, 14:15], None, ALU.mult, ALU.bypass, ("ckp", k), ("cadd", k),
               ("crest", k), name=("cks", k))

        def lo_ck(k):
            b, c = k // 2, slice((k % 2) * 128, (k % 2 + 1) * 128)
            lo(ckl[:, b % 2, c], bT[:, 0:128], ckh[:, b % 2, c], ("hi_ck", k), name=("lo_ck", k))

        def power(dst, src, *waits, name):
            tt(PO, dst, src, mh[:, 0:src.shape[1]], ALU.pow, *waits, name=name)

        def power_qk(u):
            v = 2 * (u - 4)
            power(r4[:, u % 4], ss[:, u % 4], ("veps", u), ("kscale", u - 4), ("el", v), ("el", v + 1), ("es", v),
                  ("es", v + 1), name=("r4", u))

        def power_x(t):
            power(st[:, 9:10], st[:, 8:9], ("xv", t), ("ones", 0), name=("rstd", t))

        def power_ck(k):
            power(sm[:, 14:15], sm[:, 13:14], ("cke", k), name=("ckp", k))

        def normalise_p(u, h):
            C, top_ = width(u), 128 * (u % 8 // 4 + 1)
            if h == 0 and C < top_:
                put(PO, lambda e: e.memset(P[:, u % 2, :, 256 + C:256 + top_], 0.0), ("pt", 2 * (u - 2)),
                    ("pt", 2 * (u - 2) + 1))
            pl, pc = P[:, u % 2, h, 0:nloc(u)], P[:, u % 2, h, 256:256 + C]
            ts(PO, pl, pl, rs[:, u % 4, h, 1:2], 0.5, ALU.mult, ALU.mult, ("rs", u))
            ts(PO, pc, pc, rs[:, u % 4, h, 0:1], 0.5, ALU.mult, ALU.mult, name=("norm", 2 * u + h))

        def rope_b(u):
            for k in range(2):
                d_, s_ = slice(32 * k, 32 * k + 32), slice(32 - 32 * k, 64 - 32 * k)
                tt(PO, t2[:, :, :, d_], raw[:, u % 2, :, :, s_],
                   tB[:, u % 8, :, d_].unsqueeze(1).broadcast_to([128, 2, 2, 32]), ALU.mult, ("raw", u), ("tab", 0),
                   ("add", u - 1), name=("t2", u) if k else None)

        def split(q):
            _, gi, c, _ = chunks[q]
            w = gi % 2
            if c < 4:
                h_, l_, src = wh[:, w, c, 0:512], wl[:, w, c, 0:512], wr[:, q % 2, :]
            else:
                k0 = 2 * (c - 4)
                h_, l_ = wh[:, w, k0:k0 + 2, 512:768], wl[:, w, k0:k0 + 2, 512:768]
                src = wr[:, q % 2, :].rearrange("p (k n) -> p k n", k=2)
            ts(PO, h_, src, 1.0, 1.0, ALU.mult, ALU.mult, ("w", q), ("qk", 8 * (gi - 1) - 1),
               ("v", 8 * (gi - 1) - 1), name=("sh", q))
            tt(PO, l_, src, f32(h_), ALU.subtract, ("sh", q), name=("split", q))

        def add_bo(t):
            a = acc[:, t % 8, :]
            tt(PO, a, a, bob[:, :], ALU.add, ("xacc", t), ("bo2", 0), name=("bo", t))

        first_loads()
        put(PO, lambda e: e.memset(onef[:, :], 1.0))
        put(PO, lambda e: e.memset(mh[:, :], -0.5), name=("ones", 0))
        ts(DV, isc[:, 2:4], isc[:, 0:2], 0.5, None, ALU.mult, ALU.bypass, ("const", 0), name=("half", 0))
        put(DV, lambda e: e.reciprocal(sm[:, 14:16], isc[:, 0:2]), name=("rsc", 0))
        tt(DV, isc[:, 4:5], sm[:, 14:15], sm[:, 15:16], ALU.mult, ("rsc", 0), name=("isc", 0))

        def cast_w2():
            for kt in range(KT):
                cast8(a8w[:, kt, :], b8w[:, kt, :], acc[:, kt, :], 1, ("w2raw", 0), ("half", 0), name=("c8", kt))

        def quant_w2(kt):
            quant(w2q[:, kt, :], a8w[:, kt, :], b8w[:, kt, :], qaw, qbw, ("c8", kt),
                  ("w2", kt - 1), name=("w2", kt))

        def tables():
            b8_ = [128, NT, 64]
            for j in range(2):
                w = wrow[:, j * 128:(j + 1) * 128]
                if j:
                    ts(DV, w, w, SQD, None, ALU.mult, ALU.bypass, ("table", 0), name=("wk", 0))
                tt(DV, tA[:, :, j, :], tA[:, :, j, :], w[:, 0:64].unsqueeze(1).broadcast_to(b8_), ALU.mult,
                   ("table", 0), *([("wk", 0)] if j else []))
                for k in range(2):
                    d_, s_ = slice(32 * k, 32 * k + 32), slice(32 - 32 * k, 64 - 32 * k)
                    tt(DV, tB[:, :, j, d_], tB[:, :, j, d_], w[:, s_].unsqueeze(1).broadcast_to([128, NT, 32]),
                       ALU.mult)
            w = wrow[:, 128:256]
            tt(DV, cA[:, :, :], cA[:, :, :], w[:, 0:64].unsqueeze(1).broadcast_to([128, 2, 64]), ALU.mult)
            for k in range(2):
                d_, s_ = slice(32 * k, 32 * k + 32), slice(32 - 32 * k, 64 - 32 * k)
                tt(DV, cB[:, :, d_], cB[:, :, d_], w[:, s_].unsqueeze(1).broadcast_to([128, 2, 32]), ALU.mult)
            tt(DV, wqk[:, :], wrow[:, 64:128], wrow[:, 192:256], ALU.mult, name=("tab", 0))

        def blv_out(n):
            if n == 0:
                ts(DV, blT[:, :], blT[:, :], 0.5, None, ALU.mult, ALU.bypass, ("blT", 0), name=("bl", 0))
            for h in range(4):
                mm_(bP[0][0:1, :], blT[:, 4 * n + h:4 * n + h + 1], wo4(n)[h], n + h == 0, n == 3 and h == 3,
                    ("wo4", n), ("bl", 0), name=("blvo", n) if h == 3 else None)
            if n == 3:
                put(DV, lambda e: e.tensor_copy(P[0:1, 0, 0, :], bP[0][0:1, :]), ("blvo", 3), name=("brow", 0))
                mm_(bP[1][:, :], onef[0:1, :], P[0:1, 0, 0, :], True, True, ("brow", 0), name=("ball", 0))
                tt(DV, bob[:, :], bob[:, :], bP[1][:, :], ALU.add, ("ball", 0), ("table", 0), name=("bo2", 0))

        def tile_at(s, lag):
            m = s - lag + AHEAD
            return m // 64 * 8 + m % 64 if 0 <= m < 64 * NB and m % 64 < 8 else None

        stages = {f.__name__: (kind, f) for kind, fs in (
            ("U", (tr, proj_qk, proj_v, scores, turn_p, values, out_proj, hi_qk, put_p, squares, exp_l, exp_s,
                   put_v, hi_c, kscale, lo_qk, pick, sums, inverse, put_qk, rope_a, rope_rest, eps_qk, rope_add, neg_r,
                   mask_cmp, max8, mask_max, strike, neg_max, lo_c, add_out, normalise_p, rope_b, power_qk)),
            ("T", (turn_x, entries, ffn, hi_x, cast_x, exp_w, put_et, norm_stats, normalise, lo_x, group_max, quant_x,
                   weights4, init, add_bo, power_x)),
            ("K", (ckv, turn_ck, put_kv, hi_ck, rope_ck, lo_ck, power_ck)),
            ("O", (hi_wo, lo_wo)), ("W", (split,))) for f in fs}

        def run(eng, s):
            for name, lag, *args in ORDER[eng]:
                kind, f = stages[name]
                if kind in "OW":
                    for q, c in enumerate(chunks):
                        if c[3] == s and c[0] == kind.lower():
                            f(q)
                elif kind == "U":
                    if 0 <= s - lag < NU:
                        f(s - lag, *args)
                else:
                    t = tile_at(s, lag)
                    if t is not None and (kind == "T" or t % 4 == 3):
                        f(t if kind == "T" else t // 4, *args)

        qnext = 1
        for s in range(-9, NU + 8):
            t = tile_at(s, STORE_LAG + 1)
            if 0 <= s - STORE_LAG < NU and ((s - STORE_LAG) // 8) % 8 == 7:
                store(s - STORE_LAG)
            if t is not None:
                load_acc(t)
            while qnext < len(chunks) and chunks[qnext][3] <= s + 1:
                load_chunk(qnext)
                qnext += 1
            if s % 8 == 6 and 0 < s // 8 + 1 < NU // 8:
                load_bias(s // 8 + 1)
            t = tile_at(s + 1, 0)
            if t is not None and t >= 2:
                load_x(t)
            for eng in (PE, AC, DV, PO):
                run(eng, s)
            if s == -9:
                blv_out(0)
                blv_out(1)
                cast_w2()
            if -8 <= s < -4:
                quant_w2(s + 8)
            if -8 < s < -5:
                blv_out(s + 9)
            if s == -5:
                tables()

        block = ctx.enter_context(nc.Block())

        @block.sync
        def _(e):
            qu.emit("sync", e)

        @block.tensor
        def _(e):
            qu.emit(PE, e)

        @block.scalar
        def _(e):
            qu.emit(AC, e)

        @block.vector
        def _(e):
            qu.emit(DV, e)

        @block.gpsimd
        def _(e):
            qu.emit(PO, e)


def constants():
    import numpy as np

    c = np.zeros((128, C_N), np.float32)
    r = np.arange(128)
    c[:, C_ID:C_ID + 128] = np.eye(128)
    cur = np.where(r[None, :] <= r[:, None], 0.0, NEG)
    prev = np.where(r[None, :] >= r[:, None], 0.0, NEG)
    c[:, C_MK:C_MK + 384] = np.concatenate([cur, prev, cur], 1)
    c[:, C_MG:C_MG + 128] = np.where(r[None, :] // 4 == r[:, None] // 4, 0.0, NEG)
    c[:, C_SEL:C_SEL + 32] = r[:, None] // 4 == np.arange(32)[None, :]
    c[:, C_M32:C_M32 + 32] = np.where(4 * np.arange(32)[None, :] + 3 <= r[:, None], 0.0, NEG)
    f = np.float32
    inv = f(1.0) / np.power(f(10000.0), np.arange(32, dtype=f) * f(2.0 / 64))

    def table(pos):
        ang = pos.astype(f)[:, None] * inv[None, :].astype(f)
        co, si = np.cos(ang).astype(f), np.sin(ang).astype(f)
        both = np.stack([np.concatenate([co, co], 1), np.concatenate([-si, si], 1)])
        return np.ascontiguousarray(both.reshape(2, -1, 128, 64).transpose(0, 2, 1, 3))

    return c, table(np.arange(SEQ)), table(np.arange(1, SEQ // 4 + 1) * 4 - 1)


_INS = ["hidden_states", "Wq", "bq", "Wcmp", "bcmp", "Wk", "bk", "Wv", "bv", "Wlk", "blk", "Wlv", "blv",
        "qn_w", "kn_w", "Wo", "bo"]


def kernel(**inputs):
    import numpy as _np
    import concourse.bacc as _bacc
    from concourse.bass_utils import run_bass_kernel_spmd as _run

    nc = _bacc.Bacc("TRN2", target_bir_lowering=False, num_devices=1, dynamic_dma_scratch_size=1024)
    given = {n: inputs["L0_attn_" + n] for n in _INS}
    for n in ("input2", "scale", "scale1"):
        given[n] = inputs["L0_ffn_" + n]
    given["consts"], given["tabs"], given["ctabs"] = constants()
    arrays, args = {}, []
    for name, v in given.items():
        a = _np.ascontiguousarray(v)
        a = a.reshape(1) if a.ndim == 0 else a
        arrays["in_" + name] = a
        args.append(nc.dram_tensor("in_" + name, a.shape, mybir.dt.from_np(a.dtype), kind="ExternalInput").ap())
    out = nc.dram_tensor("out_0", (NB, SEQ, HID), F32, kind="ExternalOutput").ap()
    build(nc, *args, out)
    r = _run(nc, [arrays], core_ids=[0])
    return r.results[0]["out_0"]
```
